# Optimizing a Trainium2 kernel written in Bass

```python
import numpy as np
import jax
import jax.numpy as jnp

def _softmax(x, axis=-1):
    return jax.nn.softmax(x, axis=axis)

def _gelu(x):
    return jax.nn.gelu(x, approximate=True)

def _silu(x):
    return jax.nn.silu(x)

def _sigmoid(x):
    return jax.nn.sigmoid(x)

def _layernorm(x, axis=-1, eps=1e-05):
    m = jnp.mean(x, axis=axis, keepdims=True)
    v = jnp.var(x, axis=axis, keepdims=True)
    return (x - m) / jnp.sqrt(v + eps)

def _scatter_add(tgt, idx, src, axis=0):
    return tgt.at[idx].add(src)

def _segment_sum(src, seg, n):
    return jax.ops.segment_sum(src, seg, n)
kernel_name = 'mk_perceiver_d2_seqx_r4_f9bd15'

def setup_inputs(seed: int=0):
    np.random.seed(seed)
    _w = jnp.asarray

    def _rec_inputs():
        import jax
        import jax.numpy as jnp
        _rk = jax.random.key(seed)
        x = 0.0002417 + 0.9998 * jax.random.normal(jax.random.fold_in(_rk, 1), (16, 64, 256), jnp.float32)
        _lenS = 64 - jax.random.randint(jax.random.fold_in(_rk, 7), (16,), 0, max(1, 64 // 4) + 1, jnp.int32)
        _lenS2 = 256 - jax.random.randint(jax.random.fold_in(_rk, 8), (16,), 0, max(1, 256 // 4) + 1, jnp.int32)
        _ctx_1024P = jax.random.normal(jax.random.fold_in(_rk, 11), (16, 16, 256), jnp.float32)
        _ctx_1024c = jax.random.dirichlet(jax.random.fold_in(_rk, 511), 0.3 * jnp.ones((16,), jnp.float32), (16, 256))
        _ctx_1024t = jnp.einsum('bsk,bkd->bsd', _ctx_1024c, _ctx_1024P)
        _ctx_1024t = _ctx_1024t * jax.lax.rsqrt(jnp.mean(jnp.square(_ctx_1024t)) + 1e-12) * 0.953939
        ctx_1024 = 7.22013e-05 + 1.00017 * (_ctx_1024t + 0.3 * jax.random.normal(jax.random.fold_in(_rk, 611), (16, 256, 256), jnp.float32))
        return (x, ctx_1024)
    x, ctx_1024 = _rec_inputs()

    def _L0_xattn_setup():
        import jax, jax.numpy as jnp
        import numpy as np
        EMBED = 256
        HEADS = 16
        HEAD_DIM = EMBED // HEADS
        key = jax.random.key(seed)
        ks = jax.random.split(key, 8)
        N, S, E = (4, 512, EMBED)
        s = 1.0 / np.sqrt(E)
        return {'values': jax.random.normal(ks[0], (N, S, E), jnp.float32), 'keys': jax.random.normal(ks[1], (N, S, E), jnp.float32), 'queries': jax.random.normal(ks[2], (N, S, E), jnp.float32), 'Wv': jax.random.normal(ks[3], (E, E), jnp.float32) * s, 'Wk': jax.random.normal(ks[4], (E, E), jnp.float32) * s, 'Wq': jax.random.normal(ks[5], (E, E), jnp.float32) * s, 'Wo': jax.random.normal(ks[6], (E, E), jnp.float32) * s, 'bo': jax.random.normal(ks[7], (E,), jnp.float32) * s}
    _L0_xattn_all = _L0_xattn_setup()
    _L0_xattn_in = {k: v for k, v in _L0_xattn_all.items() if k in ('Wv', 'Wk', 'Wq', 'Wo', 'bo')}
    del _L0_xattn_all

    def _L0_attn_setup():
        import jax, jax.numpy as jnp
        import numpy as np
        B, T, D, H = (4, 512, 256, 16)
        HD = D // H

        def l2_norm(x, eps=1e-12):
            return x / jnp.maximum(jnp.linalg.norm(x, axis=-1, keepdims=True), eps)
        key = jax.random.key(seed)
        ks = jax.random.split(key, 11)
        std = 0.02
        w = lambda k, shape: jax.random.normal(k, shape, jnp.float32) * std
        return dict(x=jax.random.normal(ks[0], (B, T, D), jnp.float32), Wq=w(ks[1], (D, D)), Wk=w(ks[2], (D, D)), Wv=w(ks[3], (D, D)), Wgamma=w(ks[4], (D, H)), Wf1=w(ks[5], (D, HD)), Wf2=w(ks[6], (HD, D)), Wog1=w(ks[7], (D, HD)), Wog2=w(ks[8], (HD, D)), norm_w=jnp.ones((D,), jnp.float32), Wo=w(ks[9], (D, D)))
    _L0_attn_all = _L0_attn_setup()
    _L0_attn_in = {k: v for k, v in _L0_attn_all.items() if k in ('Wq', 'Wk', 'Wv', 'Wgamma', 'Wf1', 'Wf2', 'Wog1', 'Wog2', 'norm_w', 'Wo')}
    del _L0_attn_all

    def _L0_ffn_setup():
        import jax, jax.numpy as jnp
        import numpy as np
        D_MODEL = 256
        N_HEADS = 16
        HEAD_DIM = D_MODEL // N_HEADS
        FFN_DIM = 1024
        N_EXPERTS = 8
        CAP_FRAC = 0.25
        MOE_TOKEN_DROPOUT = 0.2
        LN_EPS = 1e-05
        B, S = (4, 128)

        def _layer_norm(x, g, b):
            mu = x.mean(-1, keepdims=True)
            var = ((x - mu) ** 2).mean(-1, keepdims=True)
            return (x - mu) * jax.lax.rsqrt(var + LN_EPS) * g + b

        def _self_attention(x, wq, bq, wk, bk, wv, bv, wo, bo):
            b, s, d = x.shape
            q = ((x @ wq + bq) * HEAD_DIM ** (-0.5)).reshape(b, s, N_HEADS, HEAD_DIM)
            k = (x @ wk + bk).reshape(b, s, N_HEADS, HEAD_DIM)
            v = (x @ wv + bv).reshape(b, s, N_HEADS, HEAD_DIM)
            scores = jnp.einsum('bqhd,bkhd->bhqk', q, k)
            p = jax.nn.softmax(scores, axis=-1)
            o = jnp.einsum('bhqk,bkhd->bqhd', p, v).reshape(b, s, d)
            return o @ wo + bo

        def _moe_ffn(x, wr, w1, b1, w2, b2):
            T, D = x.shape
            C = int(np.ceil(CAP_FRAC * T))
            logits = x @ wr
            probs = jax.nn.softmax(logits, axis=-1)
            top1 = jnp.argmax(probs, axis=-1)
            m1 = jax.nn.one_hot(top1, N_EXPERTS, dtype=x.dtype)
            top2 = jnp.argmax(jnp.where(m1 > 0, -jnp.inf, logits), axis=-1)
            m2 = jax.nn.one_hot(top2, N_EXPERTS, dtype=x.dtype)
            loc1 = jnp.cumsum(m1, axis=0) - 1.0
            loc2 = jnp.cumsum(m2, axis=0) - 1.0 + m1.sum(0, keepdims=True)
            m1 = m1 * (loc1 < C)
            m2 = m2 * (loc2 < C)
            t1 = (probs * m1).sum(-1)
            t2 = (probs * m2).sum(-1)
            denom = jnp.maximum(t1 + t2, jnp.finfo(x.dtype).eps)
            t1, t2 = (t1 / denom, t2 / denom)
            tok = jnp.arange(T)
            s1 = loc1[tok, top1].astype(jnp.int32)
            s2 = loc2[tok, top2].astype(jnp.int32)
            v1 = m1[tok, top1] > 0
            v2 = m2[tok, top2] > 0
            s1 = jnp.where(v1, s1, C)
            s2 = jnp.where(v2, s2, C)
            buf = jnp.zeros((N_EXPERTS, C, D), x.dtype)
            buf = buf.at[top1, s1].set(x, mode='drop')
            buf = buf.at[top2, s2].set(x, mode='drop')
            h = jax.nn.relu(jnp.einsum('ecd,edf->ecf', buf, w1) + b1[:, None, :])
            y = (jnp.einsum('ecf,efd->ecd', h, w2) + b2[:, None, :]) * (1.0 - MOE_TOKEN_DROPOUT)
            y1 = y[top1, jnp.minimum(s1, C - 1)]
            y2 = y[top2, jnp.minimum(s2, C - 1)]
            g1 = t1 * v1
            g2 = t2 * v2
            return g1[:, None] * y1 + g2[:, None] * y2
        key = jax.random.key(seed)
        ks = jax.random.split(key, 20)

        def w(k, shape, scale=0.02):
            return jax.random.normal(k, shape, jnp.float32) * scale
        return {'x': jax.random.normal(ks[0], (B, S, D_MODEL), jnp.float32), 'wq': w(ks[1], (D_MODEL, D_MODEL)), 'bq': w(ks[2], (D_MODEL,)), 'wk': w(ks[3], (D_MODEL, D_MODEL)), 'bk': w(ks[4], (D_MODEL,)), 'wv': w(ks[5], (D_MODEL, D_MODEL)), 'bv': w(ks[6], (D_MODEL,)), 'wo': w(ks[7], (D_MODEL, D_MODEL)), 'bo': w(ks[8], (D_MODEL,)), 'ln1_g': 1.0 + w(ks[9], (D_MODEL,)), 'ln1_b': w(ks[10], (D_MODEL,)), 'ln2_g': 1.0 + w(ks[11], (D_MODEL,)), 'ln2_b': w(ks[12], (D_MODEL,)), 'wr': w(ks[13], (D_MODEL, N_EXPERTS)), 'w1': w(ks[14], (N_EXPERTS, D_MODEL, FFN_DIM)), 'b1': w(ks[15], (N_EXPERTS, FFN_DIM)), 'w2': w(ks[16], (N_EXPERTS, FFN_DIM, D_MODEL)), 'b2': w(ks[17], (N_EXPERTS, D_MODEL))}
    _L0_ffn_all = _L0_ffn_setup()
    _L0_ffn_in = {k: v for k, v in _L0_ffn_all.items() if k in ('wq', 'bq', 'wk', 'bk', 'wv', 'bv', 'wo', 'bo', 'ln1_g', 'ln1_b', 'ln2_g', 'ln2_b', 'wr', 'w1', 'b1', 'w2', 'b2')}
    del _L0_ffn_all

    def _L1_xattn_setup():
        import jax, jax.numpy as jnp
        import numpy as np
        HEADS = 16
        key = jax.random.key(seed)
        k1, k2, k3, k4 = jax.random.split(key, 4)
        B, T, S, W = (2, 512, 512, 256)
        x = jax.random.normal(k1, (B, T, W), dtype=jnp.float32)
        cond_k = jax.random.normal(k2, (B, S, W), dtype=jnp.float32)
        cond_v = jax.random.normal(k3, (B, S, W), dtype=jnp.float32)
        w_proj = jax.random.normal(k4, (W, W), dtype=jnp.float32) * 0.02
        b_proj = jnp.zeros((W,), dtype=jnp.float32)
        return {'x': x, 'cond_k': cond_k, 'cond_v': cond_v, 'w_proj': w_proj, 'b_proj': b_proj}
    _L1_xattn_all = _L1_xattn_setup()
    _L1_xattn_in = {k: v for k, v in _L1_xattn_all.items() if k in ('w_proj', 'b_proj')}
    del _L1_xattn_all

    def _L1_attn_setup():
        import jax, jax.numpy as jnp
        import numpy as np
        D_MODEL, N_HEADS = (256, 16)
        D_H = D_MODEL // N_HEADS
        D_HR = D_H // 2
        D_LATENT = 64
        THETA = 10000.0

        def rope(x, theta=THETA):
            S, d = (x.shape[-2], x.shape[-1])
            inv = theta ** (-jnp.arange(0, d, 2, dtype=jnp.float32) / d)
            ang = jnp.arange(S, dtype=jnp.float32)[:, None] * inv
            cos, sin = (jnp.cos(ang), jnp.sin(ang))
            x1, x2 = (x[..., 0::2], x[..., 1::2])
            r1 = x1 * cos - x2 * sin
            r2 = x1 * sin + x2 * cos
            return jnp.stack([r1, r2], axis=-1).reshape(x.shape)
        key = jax.random.key(seed)
        ks = jax.random.split(key, 9)
        s = lambda fan_in: 1.0 / np.sqrt(fan_in)
        return {'x': jax.random.normal(ks[0], (4, 512, D_MODEL), jnp.float32), 'W_DQ': jax.random.normal(ks[1], (D_MODEL, D_LATENT), jnp.float32) * s(D_MODEL), 'W_UQ': jax.random.normal(ks[2], (D_LATENT, N_HEADS * D_H), jnp.float32) * s(D_LATENT), 'W_QR': jax.random.normal(ks[3], (D_LATENT, N_HEADS * D_HR), jnp.float32) * s(D_LATENT), 'W_DKV': jax.random.normal(ks[4], (D_MODEL, D_LATENT), jnp.float32) * s(D_MODEL), 'W_UK': jax.random.normal(ks[5], (D_LATENT, N_HEADS * D_H), jnp.float32) * s(D_LATENT), 'W_UV': jax.random.normal(ks[6], (D_LATENT, N_HEADS * D_H), jnp.float32) * s(D_LATENT), 'W_KR': jax.random.normal(ks[7], (D_MODEL, D_HR), jnp.float32) * s(D_MODEL), 'W_O': jax.random.normal(ks[8], (N_HEADS * D_H, D_MODEL), jnp.float32) * s(N_HEADS * D_H)}
    _L1_attn_all = _L1_attn_setup()
    _L1_attn_in = {k: v for k, v in _L1_attn_all.items() if k in ('W_DQ', 'W_UQ', 'W_QR', 'W_DKV', 'W_UK', 'W_UV', 'W_KR', 'W_O')}
    del _L1_attn_all

    def _L1_ffn_setup():
        import jax, jax.numpy as jnp
        import numpy as np
        B, T, D, H, R, N = (16, 256, 256, 64, 64, 8)
        key = jax.random.key(seed)
        ks = jax.random.split(key, 8)
        s = lambda k, shape, fan: jax.random.normal(k, shape, jnp.float32) / np.sqrt(fan)
        return {'x': jax.random.normal(ks[0], (B, T, D), jnp.float32), 'W_base': s(ks[1], (D, D), D), 'b_base': jnp.zeros((D,), jnp.float32), 'W_enc': s(ks[2], (N, D, H), D), 'b_enc': jnp.zeros((N, H), jnp.float32), 'W_dec': s(ks[3], (N, H, D), H), 'b_dec': jnp.zeros((N, D), jnp.float32), 'W_down': s(ks[4], (N, D, R), D), 'b_down': jnp.zeros((N, R), jnp.float32), 'W_up': s(ks[5], (N, R, D), R), 'b_up': jnp.zeros((N, D), jnp.float32), 'connected_idx': jnp.arange(N, dtype=jnp.int32)}
    _L1_ffn_all = _L1_ffn_setup()
    _L1_ffn_in = {k: v for k, v in _L1_ffn_all.items() if k in ('W_base', 'b_base', 'W_enc', 'b_enc', 'W_dec', 'b_dec', 'W_down', 'b_down', 'W_up', 'b_up', 'connected_idx')}
    del _L1_ffn_all
    return {'x': x, 'ctx_1024': ctx_1024, 'L0_xattn_Wv': _L0_xattn_in['Wv'], 'L0_xattn_Wk': _L0_xattn_in['Wk'], 'L0_xattn_Wq': _L0_xattn_in['Wq'], 'L0_xattn_Wo': _L0_xattn_in['Wo'], 'L0_xattn_bo': _L0_xattn_in['bo'], 'L0_attn_Wq': _L0_attn_in['Wq'], 'L0_attn_Wk': _L0_attn_in['Wk'], 'L0_attn_Wv': _L0_attn_in['Wv'], 'L0_attn_Wgamma': _L0_attn_in['Wgamma'], 'L0_attn_Wf1': _L0_attn_in['Wf1'], 'L0_attn_Wf2': _L0_attn_in['Wf2'], 'L0_attn_Wog1': _L0_attn_in['Wog1'], 'L0_attn_Wog2': _L0_attn_in['Wog2'], 'L0_attn_norm_w': _L0_attn_in['norm_w'], 'L0_attn_Wo': _L0_attn_in['Wo'], 'L0_ffn_wq': _L0_ffn_in['wq'], 'L0_ffn_bq': _L0_ffn_in['bq'], 'L0_ffn_wk': _L0_ffn_in['wk'], 'L0_ffn_bk': _L0_ffn_in['bk'], 'L0_ffn_wv': _L0_ffn_in['wv'], 'L0_ffn_bv': _L0_ffn_in['bv'], 'L0_ffn_wo': _L0_ffn_in['wo'], 'L0_ffn_bo': _L0_ffn_in['bo'], 'L0_ffn_ln1_g': _L0_ffn_in['ln1_g'], 'L0_ffn_ln1_b': _L0_ffn_in['ln1_b'], 'L0_ffn_ln2_g': _L0_ffn_in['ln2_g'], 'L0_ffn_ln2_b': _L0_ffn_in['ln2_b'], 'L0_ffn_wr': _L0_ffn_in['wr'], 'L0_ffn_w1': _L0_ffn_in['w1'], 'L0_ffn_b1': _L0_ffn_in['b1'], 'L0_ffn_w2': _L0_ffn_in['w2'], 'L0_ffn_b2': _L0_ffn_in['b2'], 'L1_xattn_w_proj': _L1_xattn_in['w_proj'], 'L1_xattn_b_proj': _L1_xattn_in['b_proj'], 'L1_attn_W_DQ': _L1_attn_in['W_DQ'], 'L1_attn_W_UQ': _L1_attn_in['W_UQ'], 'L1_attn_W_QR': _L1_attn_in['W_QR'], 'L1_attn_W_DKV': _L1_attn_in['W_DKV'], 'L1_attn_W_UK': _L1_attn_in['W_UK'], 'L1_attn_W_UV': _L1_attn_in['W_UV'], 'L1_attn_W_KR': _L1_attn_in['W_KR'], 'L1_attn_W_O': _L1_attn_in['W_O'], 'L1_ffn_W_base': _L1_ffn_in['W_base'], 'L1_ffn_b_base': _L1_ffn_in['b_base'], 'L1_ffn_W_enc': _L1_ffn_in['W_enc'], 'L1_ffn_b_enc': _L1_ffn_in['b_enc'], 'L1_ffn_W_dec': _L1_ffn_in['W_dec'], 'L1_ffn_b_dec': _L1_ffn_in['b_dec'], 'L1_ffn_W_down': _L1_ffn_in['W_down'], 'L1_ffn_b_down': _L1_ffn_in['b_down'], 'L1_ffn_W_up': _L1_ffn_in['W_up'], 'L1_ffn_b_up': _L1_ffn_in['b_up'], 'L1_ffn_connected_idx': _L1_ffn_in['connected_idx']}

def reference(x, ctx_1024, L0_xattn_Wv, L0_xattn_Wk, L0_xattn_Wq, L0_xattn_Wo, L0_xattn_bo, L0_attn_Wq, L0_attn_Wk, L0_attn_Wv, L0_attn_Wgamma, L0_attn_Wf1, L0_attn_Wf2, L0_attn_Wog1, L0_attn_Wog2, L0_attn_norm_w, L0_attn_Wo, L0_ffn_wq, L0_ffn_bq, L0_ffn_wk, L0_ffn_bk, L0_ffn_wv, L0_ffn_bv, L0_ffn_wo, L0_ffn_bo, L0_ffn_ln1_g, L0_ffn_ln1_b, L0_ffn_ln2_g, L0_ffn_ln2_b, L0_ffn_wr, L0_ffn_w1, L0_ffn_b1, L0_ffn_w2, L0_ffn_b2, L1_xattn_w_proj, L1_xattn_b_proj, L1_attn_W_DQ, L1_attn_W_UQ, L1_attn_W_QR, L1_attn_W_DKV, L1_attn_W_UK, L1_attn_W_UV, L1_attn_W_KR, L1_attn_W_O, L1_ffn_W_base, L1_ffn_b_base, L1_ffn_W_enc, L1_ffn_b_enc, L1_ffn_W_dec, L1_ffn_b_dec, L1_ffn_W_down, L1_ffn_b_down, L1_ffn_W_up, L1_ffn_b_up, L1_ffn_connected_idx):
    import jax
    import jax.numpy as jnp

    def _L0_xattn_ref(values, keys, queries, Wv, Wk, Wq, Wo, bo):
        import jax, jax.numpy as jnp
        import numpy as np
        EMBED = 256
        HEADS = 16
        HEAD_DIM = EMBED // HEADS
        N = queries.shape[0]
        H, D, E = (HEADS, HEAD_DIM, EMBED)
        v = (values @ Wv.T).reshape(N, -1, H, D)
        k = (keys @ Wk.T).reshape(N, -1, H, D)
        q = (queries @ Wq.T).reshape(N, -1, H, D)
        energy = jnp.einsum('nqhd,nkhd->nhqk', q, k)
        attn = jax.nn.softmax(energy / jnp.sqrt(jnp.float32(E)), axis=3)
        out = jnp.einsum('nhql,nlhd->nqhd', attn, v).reshape(N, -1, H * D)
        return out @ Wo.T + bo

    def _L0_attn_ref(x, Wq, Wk, Wv, Wgamma, Wf1, Wf2, Wog1, Wog2, norm_w, Wo):
        import jax, jax.numpy as jnp
        import numpy as np
        B, T, D, H = (4, 512, 256, 16)
        HD = D // H

        def l2_norm(x, eps=1e-12):
            return x / jnp.maximum(jnp.linalg.norm(x, axis=-1, keepdims=True), eps)
        b, n, d = x.shape
        q = jax.nn.silu(x @ Wq)
        k = jax.nn.silu(x @ Wk)
        v = x @ Wv
        log_f = jax.nn.log_sigmoid(x @ Wf1 @ Wf2)
        gamma = -jax.nn.sigmoid(x @ Wgamma)
        q = q.reshape(b, n, H, HD)
        k = l2_norm(k.reshape(b, n, H, HD))
        v = v.reshape(b, n, H, HD)
        gk = log_f.reshape(b, n, H, HD)
        a = k * gamma[..., None] * jnp.exp(gk)

        def step(S, inp):
            qt, kt, vt, at, gkt = inp
            S = S * jnp.exp(gkt)[..., None]
            sab = jnp.einsum('bhk,bhkv->bhv', at, S)
            S = S + kt[..., None] * (sab[..., None, :] + vt[..., None, :])
            ot = jnp.einsum('bhk,bhkv->bhv', qt, S)
            return (S, ot)
        seq = tuple((jnp.moveaxis(t, 1, 0) for t in (q, k, v, a, gk)))
        S0 = jnp.zeros((b, H, HD, HD), x.dtype)
        _, o = jax.lax.scan(step, S0, seq)
        o = jnp.moveaxis(o, 0, 1).reshape(b, n, d)
        o = o * jax.nn.sigmoid(x @ Wog1 @ Wog2)
        mu = o.mean(-1, keepdims=True)
        var = ((o - mu) ** 2).mean(-1, keepdims=True)
        o = (o - mu) * jax.lax.rsqrt(var + 1e-05) * norm_w
        return o @ Wo

    def _L0_ffn_ref(x, wq, bq, wk, bk, wv, bv, wo, bo, ln1_g, ln1_b, ln2_g, ln2_b, wr, w1, b1, w2, b2):
        import jax, jax.numpy as jnp
        import numpy as np
        D_MODEL = 256
        N_HEADS = 16
        HEAD_DIM = D_MODEL // N_HEADS
        FFN_DIM = 1024
        N_EXPERTS = 8
        CAP_FRAC = 0.25
        MOE_TOKEN_DROPOUT = 0.2
        LN_EPS = 1e-05
        B, S = (4, 128)

        def _layer_norm(x, g, b):
            mu = x.mean(-1, keepdims=True)
            var = ((x - mu) ** 2).mean(-1, keepdims=True)
            return (x - mu) * jax.lax.rsqrt(var + LN_EPS) * g + b

        def _self_attention(x, wq, bq, wk, bk, wv, bv, wo, bo):
            b, s, d = x.shape
            q = ((x @ wq + bq) * HEAD_DIM ** (-0.5)).reshape(b, s, N_HEADS, HEAD_DIM)
            k = (x @ wk + bk).reshape(b, s, N_HEADS, HEAD_DIM)
            v = (x @ wv + bv).reshape(b, s, N_HEADS, HEAD_DIM)
            scores = jnp.einsum('bqhd,bkhd->bhqk', q, k)
            p = jax.nn.softmax(scores, axis=-1)
            o = jnp.einsum('bhqk,bkhd->bqhd', p, v).reshape(b, s, d)
            return o @ wo + bo

        def _moe_ffn(x, wr, w1, b1, w2, b2):
            T, D = x.shape
            C = int(np.ceil(CAP_FRAC * T))
            logits = x @ wr
            probs = jax.nn.softmax(logits, axis=-1)
            top1 = jnp.argmax(probs, axis=-1)
            m1 = jax.nn.one_hot(top1, N_EXPERTS, dtype=x.dtype)
            top2 = jnp.argmax(jnp.where(m1 > 0, -jnp.inf, logits), axis=-1)
            m2 = jax.nn.one_hot(top2, N_EXPERTS, dtype=x.dtype)
            loc1 = jnp.cumsum(m1, axis=0) - 1.0
            loc2 = jnp.cumsum(m2, axis=0) - 1.0 + m1.sum(0, keepdims=True)
            m1 = m1 * (loc1 < C)
            m2 = m2 * (loc2 < C)
            t1 = (probs * m1).sum(-1)
            t2 = (probs * m2).sum(-1)
            denom = jnp.maximum(t1 + t2, jnp.finfo(x.dtype).eps)
            t1, t2 = (t1 / denom, t2 / denom)
            tok = jnp.arange(T)
            s1 = loc1[tok, top1].astype(jnp.int32)
            s2 = loc2[tok, top2].astype(jnp.int32)
            v1 = m1[tok, top1] > 0
            v2 = m2[tok, top2] > 0
            s1 = jnp.where(v1, s1, C)
            s2 = jnp.where(v2, s2, C)
            buf = jnp.zeros((N_EXPERTS, C, D), x.dtype)
            buf = buf.at[top1, s1].set(x, mode='drop')
            buf = buf.at[top2, s2].set(x, mode='drop')
            h = jax.nn.relu(jnp.einsum('ecd,edf->ecf', buf, w1) + b1[:, None, :])
            y = (jnp.einsum('ecf,efd->ecd', h, w2) + b2[:, None, :]) * (1.0 - MOE_TOKEN_DROPOUT)
            y1 = y[top1, jnp.minimum(s1, C - 1)]
            y2 = y[top2, jnp.minimum(s2, C - 1)]
            g1 = t1 * v1
            g2 = t2 * v2
            return g1[:, None] * y1 + g2[:, None] * y2
        h = _layer_norm(x, ln1_g, ln1_b)
        h = _self_attention(h, wq, bq, wk, bk, wv, bv, wo, bo)
        x = x + h
        h = _layer_norm(x, ln2_g, ln2_b)
        b, s, d = h.shape
        moe = _moe_ffn(h.reshape(b * s, d), wr, w1, b1, w2, b2).reshape(b, s, d)
        return x + moe

    def _L1_xattn_ref(x, cond_k, cond_v, w_proj, b_proj):
        import jax, jax.numpy as jnp
        import numpy as np
        HEADS = 16
        B, T, W = x.shape
        S = cond_k.shape[1]
        H = HEADS
        d = W // H
        scale = 1.0 / jnp.sqrt(jnp.sqrt(jnp.float32(d)))
        q = x.reshape(B, T, H, d) * scale
        k = cond_k.reshape(B, S, H, d) * scale
        v = cond_v.reshape(B, S, H, d)
        scores = jnp.einsum('bthd,bshd->bhts', q, k)
        w = jax.nn.softmax(scores.astype(jnp.float32), axis=-1).astype(scores.dtype)
        out = jnp.einsum('bhts,bshd->bthd', w, v).reshape(B, T, W)
        return out @ w_proj.T + b_proj

    def _L1_attn_ref(x, W_DQ, W_UQ, W_QR, W_DKV, W_UK, W_UV, W_KR, W_O):
        import jax, jax.numpy as jnp
        import numpy as np
        D_MODEL, N_HEADS = (256, 16)
        D_H = D_MODEL // N_HEADS
        D_HR = D_H // 2
        D_LATENT = 64
        THETA = 10000.0

        def rope(x, theta=THETA):
            S, d = (x.shape[-2], x.shape[-1])
            inv = theta ** (-jnp.arange(0, d, 2, dtype=jnp.float32) / d)
            ang = jnp.arange(S, dtype=jnp.float32)[:, None] * inv
            cos, sin = (jnp.cos(ang), jnp.sin(ang))
            x1, x2 = (x[..., 0::2], x[..., 1::2])
            r1 = x1 * cos - x2 * sin
            r2 = x1 * sin + x2 * cos
            return jnp.stack([r1, r2], axis=-1).reshape(x.shape)
        B, S, _ = x.shape
        d_qk = D_H + D_HR
        c_q = x @ W_DQ
        Qc = (c_q @ W_UQ).reshape(B, S, N_HEADS, D_H).transpose(0, 2, 1, 3)
        Qr = (c_q @ W_QR).reshape(B, S, N_HEADS, D_HR).transpose(0, 2, 1, 3)
        Qr = rope(Qr)
        c_kv = x @ W_DKV
        Kc = (c_kv @ W_UK).reshape(B, S, N_HEADS, D_H).transpose(0, 2, 1, 3)
        Kr = rope((x @ W_KR)[:, None, :, :])
        Kr = jnp.broadcast_to(Kr, (B, N_HEADS, S, D_HR))
        V = (c_kv @ W_UV).reshape(B, S, N_HEADS, D_H).transpose(0, 2, 1, 3)
        Q = jnp.concatenate([Qc, Qr], axis=-1)
        K = jnp.concatenate([Kc, Kr], axis=-1)
        scores = jnp.einsum('bhqd,bhkd->bhqk', Q, K)
        scores = jnp.clip(scores, -80.0, 80.0)
        causal = jnp.tril(jnp.ones((S, S), dtype=bool))
        scores = jnp.where(causal, scores, -jnp.inf)
        weights = jax.nn.softmax(scores / jnp.sqrt(jnp.float32(d_qk)), axis=-1)
        attn = jnp.einsum('bhqk,bhkd->bhqd', weights, V)
        attn = attn.transpose(0, 2, 1, 3).reshape(B, S, N_HEADS * D_H)
        return attn @ W_O

    def _L1_ffn_ref(x, W_base, b_base, W_enc, b_enc, W_dec, b_dec, W_down, b_down, W_up, b_up, connected_idx):
        import jax, jax.numpy as jnp
        import numpy as np
        B, T, D, H, R, N = (16, 256, 256, 64, 64, 8)
        base = jnp.einsum('btd,de->bte', x, W_base) + b_base
        h = jax.nn.relu(jnp.einsum('btd,ndh->nbth', x, W_enc) + b_enc[:, None, None, :])
        recon = jnp.einsum('nbth,nhd->nbtd', h, W_dec) + b_dec[:, None, None, :]
        losses = jnp.mean((recon - x[None]) ** 2, axis=(2, 3))
        top1 = jnp.argmin(losses, axis=0)
        adp = connected_idx[top1]
        Wd, bd = (W_down[adp], b_down[adp])
        Wu, bu = (W_up[adp], b_up[adp])
        mid = jax.nn.relu(jnp.einsum('btd,bdr->btr', x, Wd) + bd[:, None, :])
        adapter_out = jnp.einsum('btr,brd->btd', mid, Wu) + bu[:, None, :]
        return base + adapter_out
    x = x + _L0_xattn_ref(ctx_1024, ctx_1024, _layernorm(x, axis=-1), L0_xattn_Wv, L0_xattn_Wk, L0_xattn_Wq, L0_xattn_Wo, L0_xattn_bo)
    x = x + _L0_attn_ref(_layernorm(x, axis=-1), L0_attn_Wq, L0_attn_Wk, L0_attn_Wv, L0_attn_Wgamma, L0_attn_Wf1, L0_attn_Wf2, L0_attn_Wog1, L0_attn_Wog2, L0_attn_norm_w, L0_attn_Wo)
    x = x + _L0_ffn_ref(_layernorm(x, axis=-1), L0_ffn_wq, L0_ffn_bq, L0_ffn_wk, L0_ffn_bk, L0_ffn_wv, L0_ffn_bv, L0_ffn_wo, L0_ffn_bo, L0_ffn_ln1_g, L0_ffn_ln1_b, L0_ffn_ln2_g, L0_ffn_ln2_b, L0_ffn_wr, L0_ffn_w1, L0_ffn_b1, L0_ffn_w2, L0_ffn_b2)
    x = x + _L1_xattn_ref(_layernorm(x, axis=-1), ctx_1024, ctx_1024, L1_xattn_w_proj, L1_xattn_b_proj)
    x = x + _L1_attn_ref(_layernorm(x, axis=-1), L1_attn_W_DQ, L1_attn_W_UQ, L1_attn_W_QR, L1_attn_W_DKV, L1_attn_W_UK, L1_attn_W_UV, L1_attn_W_KR, L1_attn_W_O)
    x = x + _L1_ffn_ref(_layernorm(x, axis=-1), L1_ffn_W_base, L1_ffn_b_base, L1_ffn_W_enc, L1_ffn_b_enc, L1_ffn_W_dec, L1_ffn_b_dec, L1_ffn_W_down, L1_ffn_b_down, L1_ffn_W_up, L1_ffn_b_up, L1_ffn_connected_idx)
    return x

_drawn_inputs = setup_inputs


def setup_inputs(seed=0):
    import zlib

    import numpy as np

    out = dict(_drawn_inputs(seed))
    spreads = {'L0_attn_norm_w': (1.0, 0.2),
     'L1_xattn_b_proj': (0.0, 0.1),
     'L1_ffn_b_base': (0.0, 0.1),
     'L1_ffn_b_enc': (0.0, 0.1),
     'L1_ffn_b_dec': (0.0, 0.1),
     'L1_ffn_b_down': (0.0, 0.302),
     'L1_ffn_b_up': (0.0, 0.1)}
    factors = {'L0_attn_Wgamma': 8.0,
     'L0_attn_Wf1': 8.0,
     'L0_attn_Wf2': 8.0,
     'L0_attn_Wog1': 8.0,
     'L0_attn_Wog2': 8.0,
     'L0_ffn_wq': 8.0,
     'L0_ffn_bq': 8.0,
     'L0_ffn_wk': 8.0,
     'L0_ffn_bk': 64.0,
     'L0_ffn_bv': 8.0,
     'L0_ffn_ln1_g': 8.0,
     'L0_ffn_ln1_b': 8.0,
     'L0_ffn_ln2_g': 8.0,
     'L0_ffn_ln2_b': 8.0,
     'L0_ffn_b1': 22.768,
     'L0_ffn_b2': 8.0}
    for name, (base, spread) in spreads.items():
        noise = np.random.default_rng([zlib.crc32(name.encode()), seed]).standard_normal(out[name].shape)
        drawn = base * np.exp(spread * noise) if base else spread * noise
        out[name] = jnp.asarray(drawn.astype(out[name].dtype))
    for name, factor in factors.items():
        out[name] = (out[name] * factor).astype(out[name].dtype)
    return out
```

```python
from contextlib import ExitStack

import concourse.bass as bass
from concourse import mybir

ALU = mybir.AluOpType
ACT = mybir.ActivationFunctionType
F32 = mybir.dt.float32
BF16 = mybir.dt.bfloat16
I32 = mybir.dt.int32
U32 = mybir.dt.uint32
AX = mybir.AxisListType

P = 128
B = 16
T = 64
S = 256
D = 256
H = 16
HD = D // H
KD = D // P
TOK = B * T
NT = TOK // P
HH = H // KD
VA = HD + 1
EPS = 1e-5
ONE = 1
FP32_EPS = 2.0 ** -23
DROPOUT = 0.2


class Scope:

    pool = []
    ended = []
    whole = None

    def __init__(self, nc, stage):
        self.nc, self.stage, self.stack, self.sems = nc, stage, ExitStack(), []

    def __enter__(self):
        self.stack.__enter__()
        return self

    def __exit__(self, *why):
        Scope.ended += self.sems
        return self.stack.__exit__(*why)

    def sb(self, name, shape, dtype=F32):
        return self.stack.enter_context(self.nc.sbuf_tensor(f"{self.stage}_{name}", shape, dtype))

    def ps(self, name, shape, dtype=F32):
        return self.stack.enter_context(self.nc.psum_tensor(f"{self.stage}_{name}", shape, dtype))

    def sem(self, name):
        self.sems.append(Scope.pool.pop(0))
        return self.sems[-1]

    def gather_sem(self, name):
        return Scope.whole.enter_context(self.nc.semaphore(f"{self.stage}_{name}"))

    def block(self):
        ended, Scope.ended = Scope.ended, []
        nums = sorted(sem.num for sem in ended)
        while nums:
            n = 1
            while n < len(nums) and nums[n] == nums[0] + n:
                n += 1
            self.nc.sync.sem_clear(range(nums[0], nums[0] + n))
            nums = nums[n:]
        for sem in ended:
            self.nc.sync.sem_inc(sem, ONE)
        Scope.pool += ended
        return self.nc.Block()


POOL = 96


def start_semaphores(nc, stack):
    Scope.pool, Scope.ended = [stack.enter_context(nc.semaphore(f"pooled{i}")) for i in range(POOL)], []
    Scope.whole = stack
    for sem in Scope.pool:
        nc.gpsimd.sem_inc(sem, ONE)


class Steps:

    def __init__(self, eng, sem, start=0):
        self.eng, self.sem, self.start, self.n = eng, sem, start, 0

    def link(self, ins):
        ins.then_inc(self.sem, 1)
        self.n += 1
        self.eng.wait_ge(self.sem, ONE + self.start + self.n)


def norm_stage(nc, stage, src, ident, eps, xnT=None, gain=None, shift=None, keep=None, product=None, heads_out=None, add_to=None):
    with Scope(nc, stage) as sc:
        stats = sc.sb("stats", [P, NT, 6])
        meanvar = sc.sb("meanvar", [P, NT, 2])
        std = sc.sb("std", [P, NT])
        rstd = sc.sb("rstd", [P, NT])
        xn = sc.sb("xn", [P, 2, D])
        xnt = sc.sb("xnt", [P, 2, KD, P])
        xnt_ps = [sc.ps(f"xnt_ps{j}", [P, KD, P]) for j in range(2)]
        y_ps = [sc.ps(f"y_ps{j}", [P, D]) for j in range(2)]
        (stats_done, var_done, std_done, rstd_done, xn_ready, xnt_mm, kept, xnt_ready, stored, y_mm, y_taken) = (sc.sem(n) for n in (
            "stats_done", "var_done", "std_done", "rstd_done", "xn_ready", "xnt_mm", "kept", "xnt_ready", "stored", "y_mm", "y_taken"))
        with sc.block() as block:

            @block.vector
            def _(dve):
                for t in range(NT):
                    nc.vector.bn_stats(stats[:, t, :], src[:, t, :]).then_inc(stats_done, 1)
                for t in range(NT):
                    dve.wait_ge(stats_done, ONE + t + 1)
                    nc.vector.bn_aggr(meanvar[:, t, :], stats[:, t, :]).then_inc(var_done, 1)
                dve.wait_ge(std_done, ONE + 1)
                nc.vector.reciprocal(rstd[:, :], std[:, :]).then_inc(rstd_done, 1)
                dve.wait_ge(rstd_done, ONE + 1)
                with dve.Fori(0, NT // 2) as two:
                    t = 2 * two

                    def take_product(j):
                        dve.wait_ge(y_mm, ONE + t + j + 1)
                        if add_to is not None:
                            row = add_to[:, bass.ds(t + j, 1), :]
                            nc.vector.tensor_tensor(row, y_ps[j][:, :], row, ALU.add).then_inc(y_taken, 1)
                        else:
                            nc.vector.tensor_copy(heads_out[:, bass.ds(t + j, 1), :, 0:HD], y_ps[j][:, :].rearrange("p (t h d) -> p t h d", t=1, h=H)).then_inc(y_taken, 1)

                    for j in range(2):
                        dve.wait_ge(xnt_mm, ONE + t)
                        if keep is not None:
                            dve.wait_ge(kept, ONE + t)
                        nc.vector.tensor_scalar(xn[:, j, :], src[:, bass.ds(t + j, 1), :], meanvar[:, bass.ds(t + j, 1), 0:1], rstd[:, bass.ds(t + j, 1)],
                                                ALU.subtract, ALU.mult).then_inc(xn_ready, 1)
                    if product is not None:
                        for j in range(2):
                            take_product(j)

            @block.gpsimd
            def _(pool):
                if keep is not None or xnT is not None:
                    with pool.Fori(0, NT // 2) as two:
                        t = 2 * two
                        for j in range(2):
                            if keep is not None:
                                pool.wait_ge(xn_ready, ONE + t + j + 1)
                                nc.gpsimd.tensor_copy(keep[:, bass.ds(t + j, 1), :], xn[:, j, :].unsqueeze(1)).then_inc(kept, 1)
                        if xnT is not None:
                            for j in range(2):
                                pool.wait_ge(xnt_ready, ONE + t + j + 1)
                                nc.gpsimd.tensor_copy(xnT[:, :, bass.ds(t * P + j * P, P)], xnt[:, j, :, :]).then_inc(stored, 1)

            @block.tensor
            def _(pe):
                with pe.Fori(0, NT // 2) as two:
                    t = 2 * two
                    for j in range(2):
                        pe.wait_ge(xn_ready, ONE + t + j + 1)
                        pe.wait_ge(xnt_ready, ONE + t)
                        for k in range(KD):
                            mm = nc.tensor.transpose(xnt_ps[j][:, k, :], xn[:, j, k * P:(k + 1) * P], ident[:, :])
                        mm.then_inc(xnt_mm, 1)
                    if product is not None:
                        weights, bias, ones = product
                        for j in range(2):
                            pe.wait_ge(xnt_ready, ONE + t + j + 1)
                            pe.wait_ge(y_taken, ONE + t)
                            for k in range(KD):
                                mm = nc.tensor.matmul(y_ps[j][:, :], xnt[:, j, k, :], weights[:, k, :], start=(k == 0), stop=(bias is None and k == KD - 1))
                            if bias is not None:
                                mm = nc.tensor.matmul(y_ps[j][:, :], ones[0:1, :], bias[0:1, :], start=False, stop=True)
                            mm.then_inc(y_mm, 1)

            @block.scalar
            def _(act):
                act.wait_ge(var_done, ONE + NT)
                nc.scalar.activation(std[:, :], meanvar[:, :, 1], ACT.Sqrt, bias=eps[:, 0:1]).then_inc(std_done, 1)
                with act.Fori(0, NT // 2) as two:
                    t = 2 * two
                    for j in range(2):
                        act.wait_ge(xnt_mm, ONE + t + j + 1)
                        if xnT is not None:
                            act.wait_ge(stored, ONE + t)
                        if product is not None:
                            act.wait_ge(y_mm, ONE + t)
                        if gain is None:
                            ins = nc.scalar.activation(xnt[:, j, :, :], xnt_ps[j][:, :, :], ACT.Copy)
                        else:
                            for k in range(KD):
                                ins = nc.scalar.activation(xnt[:, j, k, :], xnt_ps[j][:, k, :], ACT.Identity, scale=gain[:, k:k + 1], bias=shift[:, k:k + 1] if shift is not None else 0.0)
                        ins.then_inc(xnt_ready, 1)


def project_stage(nc, stage, jobs):
    N = 512
    with Scope(nc, stage) as sc:
        RING = 4
        acc = [sc.ps(f"acc{j}", [P, N]) for j in range(RING)]
        acc_mm, acc_read = sc.sem("acc_mm"), sc.sem("acc_read")
        work = [(job, slice(c * N, (c + 1) * N)) for job in jobs for c in range(TOK // N)]
        with sc.block() as block:

            @block.tensor
            def _(pe):
                for n, ((parts, outs), cols) in enumerate(work):
                    if n >= RING:
                        pe.wait_ge(acc_read, ONE + n - RING + 1)
                    for i, (w, src) in enumerate(parts):
                        mm = nc.tensor.matmul(acc[n % RING][0:outs[0][0].shape[0], :], w, src[:, cols], start=(i == 0), stop=(i == len(parts) - 1))
                    mm.then_inc(acc_mm, 1)

            @block.scalar
            def _(act):
                for n, ((parts, outs), cols) in enumerate(work):
                    act.wait_ge(acc_mm, ONE + n + 1)
                    for out, func, bias in outs:
                        ins = nc.scalar.activation(out[:, cols], acc[n % RING][0:out.shape[0], :], func, **({} if bias is None else {"bias": bias}))
                    ins.then_inc(acc_read, 1)


def half_jobs(weights, xnT, outs_of):
    return [([(weights[:, k, m * P:(m + 1) * P], xnT[:, k, :]) for k in range(KD)], outs_of(m)) for m in range(weights.shape[2] // P)]


def recurrence_inputs_stage(nc, stage, r, same_head, gate):
    N = 512
    work = [(m, slice(c * N, (c + 1) * N)) for m in range(KD) for c in range(TOK // N)]
    with Scope(nc, stage) as sc:
        square = r["a"].rearrange("p m (c n) -> p (m c) n", n=N)
        norm = r["k_sig"].rearrange("p m (c n) -> p (m c) n", n=N)
        n_ps = [sc.ps(f"n_ps{i}", [P, N]) for i in range(len(work))]
        sq_ready, n_mm, n_ready, dve_step, pool_step = (sc.sem(n) for n in ("sq_ready", "n_mm", "n_ready", "dve_step", "pool_step"))
        with sc.block() as block:

            @block.vector
            def _(dve):
                step = Steps(dve, dve_step)
                for i, (m, c) in enumerate(work):
                    step.link(nc.vector.tensor_tensor(r["k"][:, m, c], r["k"][:, m, c], r["k_sig"][:, m, c], ALU.mult))
                    nc.vector.tensor_tensor(square[:, i, :], r["k"][:, m, c], r["k"][:, m, c], ALU.mult).then_inc(sq_ready, 1)
                for i, (m, c) in enumerate(work):
                    dve.wait_ge(n_ready, ONE + i + 1)
                    step.link(nc.vector.tensor_scalar(norm[:, i, :], norm[:, i, :], 1e-12, None, ALU.max))
                    step.link(nc.vector.reciprocal(norm[:, i, :], norm[:, i, :]))
                    step.link(nc.vector.tensor_tensor(r["k"][:, m, c], r["k"][:, m, c], norm[:, i, :], ALU.mult))
                    dve.wait_ge(pool_step, ONE + 3 * (i + 1))
                    step.link(nc.vector.scalar_tensor_tensor(r["a"][:, m, c], r["k"][:, m, c], -1.0, r["gamma"][:, m, c], ALU.mult, ALU.mult))

            @block.gpsimd
            def _(pool):
                step = Steps(pool, pool_step)
                for m, c in work:
                    step.link(nc.gpsimd.tensor_tensor(r["gamma"][:, m, c], r["gamma"][:, m, c], r["f"][:, m, c], ALU.mult))
                    step.link(nc.gpsimd.tensor_tensor(r["gamma"][:, m, c], r["gamma"][:, m, c], r["f"][:, m, c], ALU.mult))
                    step.link(nc.gpsimd.tensor_tensor(r["q"][:, m, c], r["q"][:, m, c], r["q_sig"][:, m, c], ALU.mult))

            @block.tensor
            def _(pe):
                for i in range(len(work)):
                    pe.wait_ge(sq_ready, ONE + i + 1)
                    nc.tensor.matmul(n_ps[i][:, :], same_head[:, :], square[:, i, :], start=True, stop=True).then_inc(n_mm, 1)

            @block.scalar
            def _(act):
                for i in range(len(work)):
                    act.wait_ge(n_mm, ONE + i + 1)
                    nc.scalar.activation(norm[:, i, :], n_ps[i][:, :], ACT.Sqrt).then_inc(n_ready, 1)


def recurrence_stage(nc, stage, r, same_head, head_of, diag, history):
    U = 8
    TURNS = T // U
    with Scope(nc, stage) as sc:
        state = sc.sb("state", [P, KD, B, HD])
        faded = sc.sb("faded", [P, KD, B, HD])
        t_in = sc.sb("t_in", [P, KD, B, HD])
        update = sc.sb("update", [P, KD, B, HD])
        v_in = [sc.sb(f"v_in{i}", [P, KD, B, HD]) for i in range(2)]
        q_in = [sc.sb(f"q_in{i}", [P, KD, B, HD]) for i in range(2)]
        u_ps = [[sc.ps(f"u_ps{i}{m}", [P, B, HD]) for m in range(KD)] for i in range(2)]
        o_ps = sc.ps("o_ps", [P, 4, HH, U])
        cleared, t_ready, faded_ready, v_ready, u_mm, upd_ready, state_ready, q_ready, o_mm, o_taken = (sc.sem(n) for n in (
            "cleared", "t_ready", "faded_ready", "v_ready", "u_mm", "upd_ready", "state_ready", "q_ready", "o_mm", "o_taken"))

        def row(name, t, m=None):
            values = r[name].rearrange("p m (b t) -> p m b t", b=B)
            if m is None:
                return values[:, :, :, bass.ds(t, 1)].to_broadcast([P, KD, B, HD])
            return values[:, m, :, bass.ds(t, 1)].to_broadcast([P, B, HD])

        def turns(eng, body):
            with eng.Fori(0, TURNS - 1) as turn:
                body(turn, False)
            body(TURNS - 1, True)

        with sc.block() as block:

            @block.vector
            def _(dve):
                nc.vector.memset(state[:, :, :, :], 0.0).then_inc(cleared, 1)
                dve.wait_ge(cleared, ONE + 1)

                def body(turn, last):
                    for i in range(U):
                        t = U * turn + i
                        dve.wait_ge(state_ready, ONE + t)
                        for m in range(KD):
                            nc.vector.tensor_tensor(t_in[:, m, :, :], state[:, m, :, :], row("a", t, m), ALU.mult).then_inc(t_ready, 1)
                        nc.vector.tensor_tensor(faded[:, :, :, :], state[:, :, :, :], row("f", t), ALU.mult).then_inc(faded_ready, 1)
                        for m in range(KD):
                            dve.wait_ge(u_mm, ONE + 2 * t + m + 1)
                            nc.vector.tensor_tensor(update[:, m, :, :], u_ps[i % 2][m][:, :, :], row("k", t, m), ALU.mult).then_inc(upd_ready, 1)
                        dve.wait_ge(upd_ready, ONE + 2 * t + 2)
                        dve.wait_ge(faded_ready, ONE + t + 1)
                        dve.wait_ge(q_ready, ONE + t)
                        nc.vector.tensor_tensor(state[:, :, :, :], faded[:, :, :, :], update[:, :, :, :], ALU.add).then_inc(state_ready, 1)

                turns(dve, body)

            @block.gpsimd
            def _(pool):
                def value(t, i):
                    nc.gpsimd.tensor_tensor(v_in[i % 2][:, :, :, :], row("v", t), diag[:, :].unsqueeze(1).unsqueeze(1).to_broadcast([P, KD, B, HD]), ALU.mult).then_inc(v_ready, 1)

                def body(turn, last):
                    for i in range(U):
                        t = U * turn + i
                        if not (last and i == U - 1):
                            pool.wait_ge(u_mm, ONE + 2 * t)
                            value(t + 1, i + 1)
                        pool.wait_ge(state_ready, ONE + t + 1)
                        pool.wait_ge(o_mm, ONE + t - min(i, 1))
                        nc.gpsimd.tensor_tensor(q_in[i % 2][:, :, :, :], state[:, :, :, :], row("q", t), ALU.mult).then_inc(q_ready, 1)

                value(0, 0)
                turns(pool, body)

            @block.tensor
            def _(pe):
                def values(t, i):
                    pe.wait_ge(v_ready, ONE + t + 1)
                    for m in range(KD):
                        nc.tensor.matmul(u_ps[i % 2][m][:, :, :], same_head[:, :], v_in[i % 2][:, m, :, :], start=True, stop=False)

                def output(t, i):
                    pe.wait_ge(q_ready, ONE + t + 1)
                    for c in range(4):
                        mm = nc.tensor.matmul(o_ps[:, c, :, i], q_in[i % 2][:, c // 2, c % 2 * (B // 2):(c % 2 + 1) * (B // 2), :], head_of[:, :], start=True, stop=True)
                    mm.then_inc(o_mm, 1)

                def body(turn, last):
                    for i in range(U):
                        t = U * turn + i
                        for m in range(KD):
                            pe.wait_ge(t_ready, ONE + 2 * t + m + 1)
                            nc.tensor.matmul(u_ps[i % 2][m][:, :, :], same_head[:, :], t_in[:, m, :, :], start=False, stop=True).then_inc(u_mm, 1)
                        if not (last and i == U - 1):
                            pe.wait_ge(upd_ready, ONE + 2 * t)
                            values(t + 1, i + 1)
                        if i == 1:
                            pe.wait_ge(o_taken, ONE + turn)
                        if i >= 1:
                            output(t - 1, i - 1)
                    output(U * turn + U - 1, U - 1)

                values(0, 0)
                turns(pe, body)

            @block.scalar
            def _(act):
                def body(turn, last):
                    act.wait_ge(o_mm, ONE + U * turn + U)
                    nc.scalar.activation(history[:, :, :, bass.ds(U * turn, U)], o_ps[:, :, :, :], ACT.Copy).then_inc(o_taken, 1)

                turns(act, body)


def regroup_stage(nc, stage, history, ident, gate, gated):
    with Scope(nc, stage) as sc:
        h_ps = [sc.ps(f"h_ps{i}", [T, 4, B // 2, HD]) for i in range(4)]
        h_mm, h_taken = sc.sem("h_mm"), sc.sem("h_taken")
        work = [(m, bh, h4) for m in range(KD) for bh in range(2) for h4 in range(2)]
        with sc.block() as block:

            @block.tensor
            def _(pe):
                for n, (m, bh, h4) in enumerate(work):
                    if n >= 4:
                        pe.wait_ge(h_taken, ONE + n - 3)
                    for h in range(4):
                        mm = nc.tensor.transpose(h_ps[n % 4][:, h, :, :], history[:, 2 * m + bh, 4 * h4 + h, :], ident[:, :])
                    mm.then_inc(h_mm, 1)

            @block.vector
            def _(dve):
                for n, (m, bh, h4) in enumerate(work):
                    dve.wait_ge(h_mm, ONE + n + 1)
                    cols = slice(m * P + h4 * 4 * HD, m * P + (h4 + 1) * 4 * HD)
                    for j in range(2):
                        rows = slice(j * T, (j + 1) * T)
                        tiles = slice(bh * 4, bh * 4 + 4)
                        ins = nc.vector.tensor_tensor(gated[rows, tiles, cols].rearrange("p t (h d) -> p t h d", h=4),
                                                      h_ps[n % 4][:, :, j::2, :].rearrange("p h b d -> p b h d"),
                                                      gate[rows, tiles, cols].rearrange("p t (h d) -> p t h d", h=4), ALU.mult)
                    ins.then_inc(h_taken, 1)


def load_stage(nc, stage, tiles, d, loaded):
    with Scope(nc, stage) as sc:
        with sc.block() as block:

            @block.sync
            def _(sp):
                for name, tile in tiles.items():
                    src = d[name]
                    if len(tile.shape) == 3 and len(src.shape) == 2:
                        src = src.rearrange("(k p) n -> p k n", p=P)
                    sp.dma_start(tile[tuple(slice(None) for _ in tile.shape)], src).then_inc(loaded, 16)
                sp.wait_ge(loaded, ONE + 16 * len(tiles))


def fill_stage(nc, stage, tile, value):
    with Scope(nc, stage) as sc:
        filled = sc.sem("filled")
        with sc.block() as block:

            @block.gpsimd
            def _(pool):
                nc.gpsimd.memset(tile, value).then_inc(filled, 1)


def context_attention_stage(nc, stage, X, QT, head_mask, ident, ctxT_d, ctx_d, WkT, WvT, WoT, bo, ones):
    NG = 8
    with Scope(nc, stage) as sc:
        ctxT = [sc.sb(f"ctxT{j}", [P, KD, S]) for j in range(2)]
        keysT = [sc.sb(f"keysT{j}", [P, KD, S]) for j in range(2)] if WkT is not None else ctxT
        ctx = None if WkT is not None else [sc.sb(f"ctx{j}", [P, 2, S]) for j in range(2)]
        vals = [sc.sb(f"vals{j}", [P, 2, H, VA]) for j in range(2)]
        qblk = [sc.sb(f"qblk{j}", [P, KD, HH, T]) for j in range(2)]
        negmax = [sc.sb(f"negmax{j}", [P, 2]) for j in range(2)]
        prob = [sc.sb(f"prob{j}", [P, 2, S]) for j in range(2)]
        probT = [sc.sb(f"probT{j}", [P, 2, 2, P]) for j in range(2)]
        rden = sc.sb("rden", [P, 8, 2])
        heads = sc.sb("heads", [P, H, HD])
        headsT = sc.sb("headsT", [P, KD, P])
        s_ps = [sc.ps(f"s_ps{j}", [P, 2, S]) for j in range(2)]
        pt_ps = [sc.ps(f"pt_ps{j}", [P, 2, 2, P]) for j in range(2)]
        pv_ps = [sc.ps(f"pv_ps{j}", [P, 8, 2, VA]) for j in range(2)]
        a_ps = sc.ps("a_ps", [P, 512])
        b_ps = sc.ps("b_ps", [P, 512])
        ctx_in = [sc.sem(f"ctx_in{j}") for j in range(2)]
        (ones_set, k_mm, k_ready, v_mm, v_ready, q_ready, s_mm, max_ready, p_ready, pt_mm, pt_ready, pv_mm, rden_ready, o_half, o_ready,
         ot_mm, ot_ready, out_mm, x_added) = (sc.sem(n) for n in (
            "ones_set", "k_mm", "k_ready", "v_mm", "v_ready", "q_ready", "s_mm", "max_ready", "p_ready", "pt_mm", "pt_ready", "pv_mm",
            "rden_ready", "o_half", "o_ready", "ot_mm", "ot_ready", "out_mm", "x_added"))
        loads = 16 if ctx is None else 32
        with sc.block() as block:

            @block.sync
            def _(sp):
                def load(b, j):
                    sp.dma_start(ctxT[j][:, :, :], ctxT_d[bass.ds(b, 1), :, :].rearrange("b (k p) s -> p (b k) s", p=P)).then_inc(ctx_in[j], 16)
                    if ctx is not None:
                        sp.dma_start(ctx[j][:, :, :], ctx_d[bass.ds(b, 1), :, :].rearrange("b (k p) s -> p (b k) s", p=P)).then_inc(ctx_in[j], 16)
                load(0, 0)
                load(1, 1)
                with sp.Fori(1, NT) as t:
                    for j in range(2):
                        if WkT is not None:
                            sp.wait_ge(v_mm, ONE + 2 * t - 1 + j)
                        else:
                            sp.wait_ge(pv_mm, ONE + NG * t - 4 + 4 * j)
                        load(2 * t + j, j)

            @block.gpsimd
            def _(pool):
                for j in range(2):
                    nc.gpsimd.memset(vals[j][:, :, :, HD:VA], 1.0).then_inc(ones_set, 1)
                with pool.Fori(0, NT) as t:
                    for j in range(2):
                        pool.wait_ge(s_mm, ONE + NG * t)
                        for k in range(KD):
                            q = QT[:, k, bass.ds(t * P + j * T, T)]
                            nc.gpsimd.tensor_tensor(qblk[j][:, k, :, :], q.unsqueeze(1).to_broadcast([P, HH, T]),
                                                    head_mask[:, :].unsqueeze(2).to_broadcast([P, HH, T]), ALU.mult).then_inc(q_ready, 1)

            @block.tensor
            def _(pe):
                pe.wait_ge(ones_set, ONE + 2)
                with pe.Fori(0, NT) as t:
                    def project(j):
                        pe.wait_ge(ctx_in[j], ONE + loads * t + loads)
                        pe.wait_ge(ot_ready, ONE + t) if j == 0 else pe.wait_ge(k_ready, ONE + 2 * t + 1)
                        for m in range(KD):
                            for k in range(KD):
                                mm = nc.tensor.matmul(a_ps[:, m * S:(m + 1) * S], WkT[:, k, m * P:(m + 1) * P], ctxT[j][:, k, :], start=(k == 0), stop=(k == KD - 1))
                        mm.then_inc(k_mm, 1)
                        pe.wait_ge(x_added, ONE + t) if j == 0 else pe.wait_ge(v_ready, ONE + 2 * t + 1)
                        for m in range(2):
                            for k in range(KD):
                                mm = nc.tensor.matmul(b_ps[:, m * D:(m + 1) * D], ctxT[j][:, k, m * P:(m + 1) * P], WvT[:, k, :], start=(k == 0), stop=(k == KD - 1))
                        mm.then_inc(v_mm, 1)

                    def scores(g):
                        j, u = g // 4, g % 4
                        if u == 0:
                            pe.wait_ge(q_ready, ONE + 4 * t + 2 * j + 2)
                            if WkT is not None:
                                pe.wait_ge(k_ready, ONE + 2 * t + j + 1)
                            else:
                                pe.wait_ge(ctx_in[j], ONE + loads * t + loads)
                        pe.wait_ge(p_ready, ONE + NG * t + max(0, g - 1))
                        for i in range(2):
                            pair = 2 * (u % 2) + i
                            mm = nc.tensor.matmul(s_ps[g % 2][:, i, :], qblk[j][:, u // 2, 2 * pair:2 * pair + 2, :], keysT[j][:, u // 2, :], start=True, stop=True)
                        mm.then_inc(s_mm, 1)

                    def transposes(g):
                        pe.wait_ge(p_ready, ONE + NG * t + g + 1)
                        pe.wait_ge(pt_ready, ONE + NG * t + max(0, g - 1))
                        for i in range(2):
                            for c in range(2):
                                mm = nc.tensor.transpose(pt_ps[g % 2][:, i, c, :], prob[g % 2][:, i, c * P:(c + 1) * P], ident[:, :])
                        mm.then_inc(pt_mm, 1)

                    def values(g):
                        j, u = g // 4, g % 4
                        if u == 0:
                            pe.wait_ge(v_ready, ONE + 2 * t + j + 1)
                            pe.wait_ge(o_ready, ONE + 2 * t)
                        pe.wait_ge(pt_ready, ONE + NG * t + g + 1)
                        for i in range(2):
                            pair = 2 * u + i
                            for c in range(2):
                                mm = nc.tensor.matmul(pv_ps[j][:, pair, :, :], probT[g % 2][:, i, c, :], vals[j][:, c, 2 * pair:2 * pair + 2, :], start=(c == 0), stop=(c == 1))
                        mm.then_inc(pv_mm, 1)

                    for g in range(NG + 2):
                        if WkT is not None and g % 2 == 0 and g // 2 < 2:
                            project(g // 2)
                        if g < NG:
                            scores(g)
                        if 0 <= g - 1 < NG:
                            transposes(g - 1)
                        if g >= 2:
                            values(g - 2)
                    pe.wait_ge(o_ready, ONE + 2 * t + 2)
                    if WkT is not None:
                        pe.wait_ge(k_ready, ONE + 2 * t + 2)
                    pe.wait_ge(ot_ready, ONE + t)
                    for k in range(KD):
                        mm = nc.tensor.transpose(a_ps[:, k * P:(k + 1) * P], heads[:, k * HH:(k + 1) * HH, :], ident[:, :])
                    mm.then_inc(ot_mm, 1)
                    pe.wait_ge(ot_ready, ONE + t + 1)
                    if WkT is not None:
                        pe.wait_ge(v_ready, ONE + 2 * t + 2)
                    pe.wait_ge(x_added, ONE + t)
                    for k in range(KD):
                        nc.tensor.matmul(b_ps[:, 0:D], headsT[:, k, :], WoT[:, k, :], start=(k == 0), stop=False)
                    nc.tensor.matmul(b_ps[:, 0:D], ones[0:1, :], bo[0:1, :], start=False, stop=True).then_inc(out_mm, 1)

            @block.scalar
            def _(act):
                with act.Fori(0, NT) as t:
                    for g in range(NG):
                        if WkT is not None and g % 2 == 0 and g // 2 < 2:
                            j = g // 2
                            act.wait_ge(k_mm, ONE + 2 * t + j + 1)
                            act.wait_ge(s_mm, ONE + NG * t)
                            nc.scalar.activation(keysT[j][:, :, :], a_ps[:, :], ACT.Copy).then_inc(k_ready, 1)
                        if ctx is not None and g % 2 == 0 and g // 2 < 2:
                            j = g // 2
                            act.wait_ge(ctx_in[j], ONE + loads * t + loads)
                            act.wait_ge(pv_mm, ONE + NG * t)
                            nc.scalar.activation(vals[j][:, :, :, 0:HD], ctx[j][:, :, :].rearrange("p c (h d) -> p c h d", h=H), ACT.Copy).then_inc(v_ready, 1)
                        act.wait_ge(max_ready, ONE + NG * t + g + 1)
                        act.wait_ge(pt_mm, ONE + NG * t + max(0, g - 1))
                        for i in range(2):
                            ins = nc.scalar.activation(prob[g % 2][:, i, :], s_ps[g % 2][:, i, :], ACT.Exp, bias=negmax[g % 2][:, i:i + 1])
                        ins.then_inc(p_ready, 1)
                    act.wait_ge(ot_mm, ONE + t + 1)
                    act.wait_ge(out_mm, ONE + t)
                    nc.scalar.activation(headsT[:, :, :], a_ps[:, 0:D], ACT.Copy).then_inc(ot_ready, 1)

            @block.vector
            def _(dve):
                with dve.Fori(0, NT) as t:
                    def take_values(j):
                        dve.wait_ge(v_mm, ONE + 2 * t + j + 1)
                        dve.wait_ge(pv_mm, ONE + NG * t)
                        nc.vector.tensor_copy(vals[j][:, :, :, 0:HD], b_ps[:, :].rearrange("p (c h d) -> p c h d", c=2, h=H)).then_inc(v_ready, 1)

                    def take_heads(j):
                        dve.wait_ge(pv_mm, ONE + NG * t + 4 * j + 4)
                        nc.vector.reciprocal(rden[:, :, :], pv_ps[j][:, :, :, HD]).then_inc(rden_ready, 1)
                        dve.wait_ge(rden_ready, ONE + 2 * t + j + 1)
                        dve.wait_ge(ot_mm, ONE + t)
                        for e in range(2):
                            rows = slice(e * T, e * T + T)
                            ins = nc.vector.tensor_tensor(heads[j * T:j * T + T, e::2, :], pv_ps[j][rows, :, e, 0:HD],
                                                          rden[rows, :, e].unsqueeze(2).to_broadcast([T, 8, HD]), ALU.mult)
                        ins.then_inc(o_ready, 1)

                    for g in range(NG + 1):
                        if WkT is not None and g % 2 == 0 and g // 2 < 2:
                            take_values(g // 2)
                        if g < NG:
                            dve.wait_ge(s_mm, ONE + NG * t + g + 1)
                            dve.wait_ge(p_ready, ONE + NG * t + max(0, g - 1))
                            nc.vector.tensor_reduce(negmax[g % 2][:, :], s_ps[g % 2][:, :, :], AX.X, ALU.max, negate=True).then_inc(max_ready, 1)
                        if g >= 1:
                            dve.wait_ge(pt_mm, ONE + NG * t + g)
                            dve.wait_ge(pv_mm, ONE + NG * t + max(0, g - 2))
                            nc.vector.tensor_copy(probT[(g - 1) % 2][:, :, :, :], pt_ps[(g - 1) % 2][:, :, :, :]).then_inc(pt_ready, 1)
                        if g == 6:
                            take_heads(0)
                    take_heads(1)
                    dve.wait_ge(out_mm, ONE + t + 1)
                    nc.vector.tensor_tensor(X[:, bass.ds(t, 1), :], b_ps[:, 0:D], X[:, bass.ds(t, 1), :], ALU.add).then_inc(x_added, 1)


def batch_attention_stage(nc, stage, X, QT, KT, vals_all, head_mask, ident, WoT, bo, ones, clip=None, scale=1.0, causal=None):
    G = QT.shape[1]
    HG = H // G
    NU = 4
    with Scope(nc, stage) as sc:
        qblk = [sc.sb(f"qblk{u}", [P, 2, 8, T]) for u in range(NU)]
        vals = [sc.sb(f"vals{j}", [P, 2, H, VA]) for j in range(2)]
        top = [sc.sb(f"top{i}", [P, 8]) for i in range(2)]
        shifted = [sc.sb(f"shifted{i}", [P, 8, T]) for i in range(2)]
        prob = [sc.sb(f"prob{i}", [P, 8, T]) for i in range(2)]
        probT = [sc.sb(f"probT{i}", [P, 4, P]) for i in range(2)]
        rden = [sc.sb(f"rden{i}", [P, 4, 2, 2]) for i in range(2)]
        heads = [sc.sb(f"heads{j}", [P, H, HD]) for j in range(2)]
        headsT = [sc.sb(f"headsT{j}", [P, KD, P]) for j in range(2)]
        s_ps = [sc.ps(f"s_ps{i}", [P, 8, T]) for i in range(2)]
        pt_ps = [sc.ps(f"pt_ps{i}", [P, 4, P]) for i in range(2)]
        pv_ps = [sc.ps(f"pv_ps{i}", [P, 4, 2, 2, VA]) for i in range(2)]
        ot_ps = sc.ps("ot_ps", [P, KD, P])
        out_ps = sc.ps("out_ps", [P, D])
        (q_ready, vals_ready, s_mm, top_ready, shifted_ready, exp_ready, p_ready, pt_mm, pt_ready, pv_mm, rden_ready, o_ready, ot_mm, ot_ready, out_mm, x_added) = (sc.sem(n) for n in (
            "q_ready", "vals_ready", "s_mm", "top_ready", "shifted_ready", "exp_ready", "p_ready", "pt_mm", "pt_ready", "pv_mm", "rden_ready", "o_ready", "ot_mm", "ot_ready", "out_mm", "x_added"))
        prob_done = exp_ready if causal is None else p_ready
        zeroed = sc.sem("zeroed")
        with sc.block() as block:

            def unit(two, u):
                return NU * two + u

            def before(two, u):
                return NU * two + max(0, u - 1)

            @block.gpsimd
            def _(pool):
                with pool.Fori(0, NT // 2) as two:
                    for j in range(2):
                        for m in range(2):
                            u = 2 * j + m
                            pool.wait_ge(s_mm, ONE + NU * two)
                            for b in range(2):
                                for g in range(8 // HG):
                                    q = QT[:, m * (8 // HG) + g, bass.ds(two * (2 * P) + j * P + b * T, T)]
                                    ins = nc.gpsimd.tensor_tensor(qblk[u][:, b, g * HG:(g + 1) * HG, :], q.unsqueeze(1).to_broadcast([P, HG, T]),
                                                                  head_mask[:, 0:HG].unsqueeze(2).to_broadcast([P, HG, T]), ALU.mult)
                            ins.then_inc(q_ready, 1)
                    if causal is not None:
                        for u in range(NU):
                            pool.wait_ge(exp_ready, ONE + unit(two, u) + 1)
                            nc.gpsimd.tensor_tensor(prob[u % 2][:, :, :], prob[u % 2][:, :, :], causal[:, :].unsqueeze(1).to_broadcast([P, 8, T]), ALU.mult).then_inc(p_ready, 1)

            @block.tensor
            def _(pe):
                pe.wait_ge(zeroed, ONE + 4)
                with pe.Fori(0, NT // 2) as two:
                    def scores(u):
                        j, m = u // 2, u % 2
                        pe.wait_ge(q_ready, ONE + unit(two, u) + 1)
                        pe.wait_ge(shifted_ready, ONE + before(two, u))
                        for i in range(4):
                            for b in range(2):
                                mm = nc.tensor.matmul(s_ps[u % 2][:, 2 * i + b, :], qblk[u][:, b, 2 * i:2 * i + 2, :],
                                                      KT[:, m * (8 // HG) + 2 * i // HG, bass.ds(two * (2 * P) + j * P + b * T, T)], start=True, stop=True)
                        mm.then_inc(s_mm, 1)

                    def transposes(u):
                        pe.wait_ge(prob_done, ONE + unit(two, u) + 1)
                        pe.wait_ge(pt_ready, ONE + before(two, u))
                        for i in range(4):
                            mm = nc.tensor.transpose(pt_ps[u % 2][:, i, :], prob[u % 2][:, 2 * i:2 * i + 2, :], ident[:, :])
                        mm.then_inc(pt_mm, 1)

                    def values(u):
                        j, m = u // 2, u % 2
                        pe.wait_ge(vals_ready, ONE + 2 * two + j + 1)
                        pe.wait_ge(pt_ready, ONE + unit(two, u) + 1)
                        pe.wait_ge(o_ready, ONE + before(two, u))
                        for i in range(4):
                            pair = 4 * m + i
                            mm = nc.tensor.matmul(pv_ps[u % 2][:, i, :, :, :], probT[u % 2][:, i, :], vals[j][:, :, 2 * pair:2 * pair + 2, :], start=True, stop=True)
                        mm.then_inc(pv_mm, 1)

                    def output(j):
                        pe.wait_ge(o_ready, ONE + NU * two + 2 * j + 2)
                        pe.wait_ge(ot_ready, ONE + 2 * two + j)
                        for k in range(KD):
                            mm = nc.tensor.transpose(ot_ps[:, k, :], heads[j][:, k * HH:(k + 1) * HH, :], ident[:, :])
                        mm.then_inc(ot_mm, 1)
                        pe.wait_ge(ot_ready, ONE + 2 * two + j + 1)
                        pe.wait_ge(x_added, ONE + 2 * two + j)
                        for k in range(KD):
                            mm = nc.tensor.matmul(out_ps[:, :], headsT[j][:, k, :], WoT[:, k, :], start=(k == 0), stop=(bo is None and k == KD - 1))
                        if bo is not None:
                            mm = nc.tensor.matmul(out_ps[:, :], ones[0:1, :], bo[0:1, :], start=False, stop=True)
                        mm.then_inc(out_mm, 1)

                    for u in range(NU + 2):
                        if u < NU:
                            scores(u)
                        if 0 <= u - 1 < NU:
                            transposes(u - 1)
                        if u >= 2:
                            values(u - 2)
                        if u == 4:
                            output(0)
                    output(1)

            @block.scalar
            def _(act):
                with act.Fori(0, NT // 2) as two:
                    def take_heads(j):
                        act.wait_ge(ot_mm, ONE + 2 * two + j + 1)
                        act.wait_ge(out_mm, ONE + 2 * two + j)
                        nc.scalar.activation(headsT[j][:, :, :], ot_ps[:, :, :], ACT.Copy).then_inc(ot_ready, 1)

                    act.wait_ge(pv_mm, ONE + NU * two)
                    for j in range(2):
                        for b in range(2):
                            rows = slice(b * T, (b + 1) * T)
                            ins = nc.scalar.activation(vals[j][rows, b:b + 1, :, :], vals_all[rows, bass.ds(2 * two + j, 1), :, :], ACT.Copy)
                        ins.then_inc(vals_ready, 1)
                    for u in range(NU):
                        act.wait_ge(shifted_ready, ONE + unit(two, u) + 1)
                        act.wait_ge(pt_mm, ONE + before(two, u))
                        nc.scalar.activation(prob[u % 2][:, :, :], shifted[u % 2][:, :, :], ACT.Exp, scale=scale).then_inc(exp_ready, 1)
                    take_heads(0)
                    take_heads(1)

            @block.vector
            def _(dve):
                for j in range(2):
                    for b in range(2):
                        nc.vector.memset(vals[j][b * T:(b + 1) * T, 1 - b, :, :], 0.0).then_inc(zeroed, 1)
                with dve.Fori(0, NT // 2) as two:
                    def shift(u):
                        dve.wait_ge(s_mm, ONE + unit(two, u) + 1)
                        if clip is None:
                            nc.vector.tensor_reduce(top[u % 2][:, :], s_ps[u % 2][:, :, :], AX.X, ALU.max).then_inc(top_ready, 1)
                            dve.wait_ge(top_ready, ONE + unit(two, u) + 1)
                        dve.wait_ge(exp_ready, ONE + before(two, u))
                        if clip is None:
                            nc.vector.tensor_tensor(shifted[u % 2][:, :, :], s_ps[u % 2][:, :, :], top[u % 2][:, :].unsqueeze(2).to_broadcast([P, 8, T]), ALU.subtract).then_inc(shifted_ready, 1)
                        else:
                            nc.vector.tensor_scalar(shifted[u % 2][:, :, :], s_ps[u % 2][:, :, :], clip, -clip, ALU.min, ALU.max).then_inc(shifted_ready, 1)

                    def take_transposed(u):
                        dve.wait_ge(pt_mm, ONE + unit(two, u) + 1)
                        dve.wait_ge(pv_mm, ONE + before(two, u))
                        nc.vector.tensor_copy(probT[u % 2][:, :, :], pt_ps[u % 2][:, :, :]).then_inc(pt_ready, 1)

                    def take_heads(u):
                        j, m = u // 2, u % 2
                        dve.wait_ge(pv_mm, ONE + unit(two, u) + 1)
                        nc.vector.reciprocal(rden[u % 2][:, :, :, :], pv_ps[u % 2][:, :, :, :, HD]).then_inc(rden_ready, 1)
                        dve.wait_ge(rden_ready, ONE + unit(two, u) + 1)
                        dve.wait_ge(ot_mm, ONE + 2 * two)
                        for b in range(2):
                            for e in range(2):
                                rows = slice(e * T, e * T + T)
                                ins = nc.vector.tensor_tensor(heads[j][b * T:b * T + T, 8 * m + e:8 * m + 8:2, :], pv_ps[u % 2][rows, :, b, e, 0:HD],
                                                              rden[u % 2][rows, :, b, e].unsqueeze(2).to_broadcast([T, 4, HD]), ALU.mult)
                        ins.then_inc(o_ready, 1)

                    def add(j):
                        dve.wait_ge(out_mm, ONE + 2 * two + j + 1)
                        row = X[:, bass.ds(2 * two + j, 1), :]
                        nc.vector.tensor_tensor(row, out_ps[:, :], row, ALU.add).then_inc(x_added, 1)

                    for u in range(NU + 2):
                        if u < NU:
                            shift(u)
                        if 0 <= u - 1 < NU:
                            take_transposed(u - 1)
                        if u >= 2:
                            take_heads(u - 2)
                    add(0)
                    add(1)


E = 8
CAP = 256
FF = 1024
KF = FF // P
ROWS = E * CAP


def routing_stage(nc, stage, hT, wr, upto, all_ones, expert_ids, slot, slot_kept, weight):
    with Scope(nc, stage) as sc:
        logits = sc.sb("logits", [P, NT, E])
        best = sc.sb("best", [P, NT, 8])
        best_id = sc.sb("best_id", [P, NT, 8], U32)
        chosen = sc.sb("chosen", [P, NT, 2])
        onehot = sc.sb("onehot", [P, NT, 2, E])
        onehot16 = sc.sb("onehot16", [P, NT, 2, E], BF16)
        count = sc.sb("count", [P, NT, 2, E])
        place = sc.sb("place", [P, NT, 2])
        fits = sc.sb("fits", [P, NT, 2])
        shifted = sc.sb("shifted", [P, NT, E])
        expd = sc.sb("expd", [P, NT, E])
        part = sc.sb("part", [P, NT])
        top2 = sc.sb("top2", [P, NT, 2])
        row = sc.sb("row", [P, NT, 2])
        logit_ps = sc.ps("logit_ps", [P, NT, E])
        count_ps = sc.ps("count_ps", [P, NT, 2, E])
        total_ps = sc.ps("total_ps", [P, E])
        logits_mm, onehot_ready, count_mm, shift_ready, exp_ready, dve_step = (sc.sem(n) for n in ("logits_mm", "onehot_ready", "count_mm", "shift_ready", "exp_ready", "dve_step"))
        with sc.block() as block:

            @block.tensor
            def _(pe):
                for t in range(NT):
                    for k in range(KD):
                        mm = nc.tensor.matmul(logit_ps[:, t, :], hT[:, k, t * P:(t + 1) * P], wr[:, k, :], start=(k == 0), stop=(k == KD - 1))
                mm.then_inc(logits_mm, 1)
                pe.wait_ge(onehot_ready, ONE + 1)
                for t in range(NT):
                    for before in range(t + 1):
                        nc.tensor.matmul(count_ps[:, t, :, :], upto[:, :] if before == t else all_ones[:, :], onehot16[:, before, :, :], start=(before == 0), stop=(before == t))
                for t in range(NT):
                    mm = nc.tensor.matmul(total_ps[:, :], all_ones[:, :], onehot16[:, t, 0, :], start=(t == 0), stop=(t == NT - 1))
                mm.then_inc(count_mm, 1)

            @block.scalar
            def _(act):
                act.wait_ge(shift_ready, ONE + 1)
                nc.scalar.activation(expd[:, :, :], shifted[:, :, :], ACT.Exp).then_inc(exp_ready, 1)
                nc.scalar.activation(top2[:, :, :], top2[:, :, :], ACT.Exp).then_inc(exp_ready, 1)

            @block.vector
            def _(dve):
                step = Steps(dve, dve_step)
                dve.wait_ge(logits_mm, ONE + 1)
                step.link(nc.vector.tensor_copy(logits[:, :, :], logit_ps[:, :, :]))
                for t in range(NT):
                    ins = nc.vector.max(best[:, t, :], logits[:, t, :])
                step.link(ins)
                for t in range(NT):
                    ins = nc.vector.max_index(best_id[:, t, :], best[:, t, :], logits[:, t, :])
                step.link(ins)
                step.link(nc.vector.tensor_copy(chosen[:, :, :], best_id[:, :, 0:2]))
                step.link(nc.vector.tensor_tensor(onehot[:, :, :, :], chosen[:, :, :].unsqueeze(3).to_broadcast([P, NT, 2, E]),
                                                  expert_ids[:, :].unsqueeze(1).unsqueeze(1).to_broadcast([P, NT, 2, E]), ALU.is_equal))
                nc.vector.tensor_copy(onehot16[:, :, :, :], onehot[:, :, :, :]).then_inc(onehot_ready, 1)
                step.link(nc.vector.tensor_tensor(top2[:, :, :], best[:, :, 0:2], best[:, :, 0:1].to_broadcast([P, NT, 2]), ALU.subtract))
                nc.vector.tensor_tensor(shifted[:, :, :], logits[:, :, :], best[:, :, 0:1].to_broadcast([P, NT, E]), ALU.subtract).then_inc(shift_ready, 1)
                dve.wait_ge(count_mm, ONE + 1)
                step.link(nc.vector.tensor_copy(count[:, :, :, :], count_ps[:, :, :, :]))
                step.link(nc.vector.tensor_tensor(count[:, :, 1, :], count[:, :, 1, :], total_ps[:, :].unsqueeze(1).to_broadcast([P, NT, E]), ALU.add))
                step.link(nc.vector.tensor_tensor(count[:, :, :, :], count[:, :, :, :], onehot[:, :, :, :], ALU.mult))
                step.link(nc.vector.tensor_reduce(place[:, :, :], count[:, :, :, :], AX.X, ALU.add))
                step.link(nc.vector.tensor_scalar(fits[:, :, :], place[:, :, :], CAP + 0.5, None, ALU.is_lt))
                step.link(nc.vector.tensor_scalar(place[:, :, :], place[:, :, :], float(CAP), -1.0, ALU.min, ALU.add))
                step.link(nc.vector.scalar_tensor_tensor(row[:, :, :], chosen[:, :, :], float(CAP), place[:, :, :], ALU.mult, ALU.add))
                step.link(nc.vector.tensor_copy(slot[:, :, :], row[:, :, :]))
                step.link(nc.vector.scalar_tensor_tensor(row[:, :, :], fits[:, :, :], -2.0 * ROWS, row[:, :, :], ALU.mult, ALU.add))
                step.link(nc.vector.tensor_scalar(row[:, :, :], row[:, :, :], 2.0 * ROWS, None, ALU.add))
                step.link(nc.vector.tensor_copy(slot_kept[:, :, :], row[:, :, :]))
                dve.wait_ge(exp_ready, ONE + 2)
                step.link(nc.vector.tensor_reduce(part[:, :], expd[:, :, :], AX.X, ALU.add))
                step.link(nc.vector.reciprocal(part[:, :], part[:, :]))
                step.link(nc.vector.tensor_tensor(top2[:, :, :], top2[:, :, :], part[:, :].unsqueeze(2).to_broadcast([P, NT, 2]), ALU.mult))
                step.link(nc.vector.tensor_tensor(top2[:, :, :], top2[:, :, :], fits[:, :, :], ALU.mult))
                step.link(nc.vector.tensor_tensor(part[:, :], top2[:, :, 0], top2[:, :, 1], ALU.add))
                step.link(nc.vector.tensor_scalar(part[:, :], part[:, :], FP32_EPS, None, ALU.max))
                step.link(nc.vector.reciprocal(part[:, :], part[:, :]))
                step.link(nc.vector.tensor_tensor(weight[:, :, :], top2[:, :, :], part[:, :].unsqueeze(2).to_broadcast([P, NT, 2]), ALU.mult))


def scatter_stage(nc, stage, xn, slot_kept, zeros, buf_d):
    with Scope(nc, stage) as sc:
        cleared, scattered = sc.sem("cleared"), sc.gather_sem("scattered")
        with sc.block() as block:

            @block.sync
            def _(sp):
                for e in range(E):
                    sp.dma_start(buf_d[e * CAP:(e + 1) * CAP, :].rearrange("(c p) d -> p c d", p=P), zeros[:, :].rearrange("p (c d) -> p c d", c=CAP // P)).then_inc(cleared, 16)

            @block.gpsimd
            def _(pool):
                pool.wait_ge(cleared, ONE + 16 * E)
                for t in range(NT):
                    for c in range(2):
                        nc.gpsimd.indirect_dma_start(out=buf_d, out_offset=bass.IndirectOffsetOnAxis(ap=slot_kept[:, t, c:c + 1], axis=0), in_=xn[:, t, :], in_offset=None,
                                                     bounds_check=ROWS - 1, oob_is_err=False).then_inc(scattered, 16)
                pool.wait_ge(scattered, 16 * 2 * NT)


def experts_stage(nc, stage, w1_d, w2_d, buf_d, y_d, w1, w2, w_in, b1, b2, ones, gain, shift, ident):
    with Scope(nc, stage) as sc:
        rows = [sc.sb(f"rows{j}", [P, 2, D]) for j in range(2)]
        rowsT = [sc.sb(f"rowsT{j}", [P, KD, CAP]) for j in range(2)]
        hidden = [sc.sb(f"hidden{j}", [P, KF, CAP]) for j in range(2)]
        y = [sc.sb(f"y{j}", [P, 2, D]) for j in range(2)]
        xt_ps = [sc.ps(f"xt_ps{j}", [P, KD, CAP]) for j in range(2)]
        h_ps = [sc.ps(f"h_ps{j}", [P, 2, CAP]) for j in range(4)]
        y_ps = [sc.ps(f"y_ps{j}", [P, 2, D]) for j in range(2)]
        rows_in = [sc.sem(f"rows_in{j}") for j in range(2)]
        y_out = [sc.sem(f"y_out{j}") for j in range(2)]
        xt_mm, xt_ready, h_mm, h_ready, y_mm, y_ready = (sc.sem(n) for n in ("xt_mm", "xt_ready", "h_mm", "h_ready", "y_mm", "y_ready"))
        NH = KF // 2
        with sc.block() as block:

            @block.sync
            def _(sp):
                def load_rows(e2, j):
                    sp.dma_start(rows[j][:, :, :], buf_d.rearrange("(e c p) d -> p (e c) d", p=P, e=E)[:, bass.ds(e2, 2), :]).then_inc(rows_in[j], 16)

                load_rows(0, 0)
                load_rows(2, 1)
                with sp.Fori(1, E // 2) as two:
                    for j in range(2):
                        e = sp.snap(2 * two + j)
                        e2 = sp.snap(2 * e)
                        sp.wait_ge(xt_mm, ONE + e - 1)
                        load_rows(e2, j)
                        sp.wait_ge(h_mm, ONE + NH * (e - 1))
                        sp.dma_start(w1[j][:, :, :], w1_d[bass.ds(e, 1), :, :].rearrange("e (k p) f -> p (e k) f", p=P)).then_inc(w_in[j], 16)
                        sp.wait_ge(y_mm, ONE + e - 1)
                        sp.dma_start(w2[j][:, :, :], w2_d[bass.ds(e, 1), :, :].rearrange("e (k p) f -> p (e k) f", p=P)).then_inc(w_in[j], 16)

            @block.tensor
            def _(pe):
                with pe.Fori(0, E // 2) as two:
                    def turn_rows(j):
                        pe.wait_ge(rows_in[j], ONE + 16 * two + 16)
                        pe.wait_ge(xt_ready, ONE + 2 * two)
                        for k in range(KD):
                            for c in range(2):
                                mm = nc.tensor.transpose(xt_ps[j][:, k, c * P:(c + 1) * P], rows[j][:, c, k * P:(k + 1) * P], ident[:, :])
                        mm.then_inc(xt_mm, 1)

                    def first_layer(j):
                        pe.wait_ge(w_in[j], 32 * two + 32)
                        pe.wait_ge(xt_ready, ONE + 2 * two + j + 1)
                        for i in range(NH):
                            pe.wait_ge(h_ready, ONE + NH * (2 * two + j))
                            for f in range(2):
                                for k in range(KD):
                                    mm = nc.tensor.matmul(h_ps[i][:, f, :], w1[j][:, k, (2 * i + f) * P:(2 * i + f + 1) * P], rowsT[j][:, k, :], start=(k == 0), stop=(k == KD - 1))
                            mm.then_inc(h_mm, 1)

                    def second_layer(j):
                        pe.wait_ge(h_ready, ONE + NH * (2 * two + j + 1))
                        pe.wait_ge(y_ready, ONE + 2 * two)
                        for c in range(2):
                            for f in range(KF):
                                nc.tensor.matmul(y_ps[j][:, c, :], hidden[j][:, f, c * P:(c + 1) * P], w2[j][:, f, :], start=(f == 0), stop=False)
                            mm = nc.tensor.matmul(y_ps[j][:, c, :], ones[0:1, :], b2[0:1, bass.ds(2 * two + j, 1), :], start=False, stop=True)
                        mm.then_inc(y_mm, 1)

                    turn_rows(0)
                    first_layer(0)
                    turn_rows(1)
                    second_layer(0)
                    first_layer(1)
                    second_layer(1)

            @block.scalar
            def _(act):
                with act.Fori(0, E // 2) as two:
                    for j in range(2):
                        act.wait_ge(xt_mm, ONE + 2 * two + j + 1)
                        act.wait_ge(h_mm, ONE + NH * 2 * two)
                        for k in range(KD):
                            ins = nc.scalar.activation(rowsT[j][:, k, :], xt_ps[j][:, k, :], ACT.Identity, scale=gain[:, k:k + 1], bias=shift[:, k:k + 1])
                        ins.then_inc(xt_ready, 1)
                    for j in range(2):
                        act.wait_ge(y_ready, ONE + 2 * two + j + 1)
                        act.dma_start(y_d.rearrange("(e c p) d -> p (e c) d", p=P, e=E)[:, bass.ds(4 * two + 2 * j, 2), :], y[j][:, :, :]).then_inc(y_out[j], 16)
                for j in range(2):
                    act.wait_ge(y_out[j], ONE + 16 * (E // 2))

            @block.vector
            def _(dve):
                with dve.Fori(0, E // 2) as two:
                    for j in range(2):
                        dve.wait_ge(y_mm, ONE + 2 * two)
                        for i in range(NH):
                            dve.wait_ge(h_mm, ONE + NH * (2 * two + j) + i + 1)
                            for f in range(2):
                                ins = nc.vector.tensor_scalar(hidden[j][:, 2 * i + f, :], h_ps[i][:, f, :], b1[:, bass.ds(2 * two + j, 1), 2 * i + f], 0.0, ALU.add, ALU.max)
                            ins.then_inc(h_ready, 1)
                        dve.wait_ge(y_mm, ONE + 2 * two + j + 1)
                        dve.wait_ge(y_out[j], ONE + 16 * two)
                        nc.vector.tensor_scalar(y[j][:, :, :], y_ps[j][:, :, :], 1.0 - DROPOUT, None, ALU.mult).then_inc(y_ready, 1)


def combine_stage(nc, stage, X, Y, y_d, slot, weight):
    RING = 4
    with Scope(nc, stage) as sc:
        got = [sc.sb(f"got{i}", [P, D]) for i in range(RING)]
        got_in = [sc.gather_sem(f"got_in{i}") for i in range(RING)]
        used, dve_step = sc.sem("used"), sc.sem("dve_step")
        with sc.block() as block:

            @block.gpsimd
            def _(pool):
                for n in range(2 * NT):
                    if n >= RING:
                        pool.wait_ge(used, ONE + n - RING + 1)
                    nc.gpsimd.indirect_dma_start(out=got[n % RING][:, :], out_offset=None, in_=y_d,
                                                 in_offset=bass.IndirectOffsetOnAxis(ap=slot[:, n // 2, n % 2:n % 2 + 1], axis=0)).then_inc(got_in[n % RING], 16)

            @block.vector
            def _(dve):
                step = Steps(dve, dve_step)
                step.link(nc.vector.tensor_tensor(X[:, :, :], X[:, :, :], Y[:, :, :], ALU.add))
                for n in range(2 * NT):
                    dve.wait_ge(got_in[n % RING], 16 * (n // RING + 1))
                    dve.wait_ge(used, ONE + n)
                    nc.vector.scalar_tensor_tensor(X[:, n // 2, :], got[n % RING][:, :], weight[:, n // 2, n % 2:n % 2 + 1], X[:, n // 2, :], ALU.mult, ALU.add).then_inc(used, 1)


def token_product_stage(nc, stage, srcT, weights, out, func):
    with Scope(nc, stage) as sc:
        y_ps = [sc.ps(f"y_ps{i}", [P, 2, D]) for i in range(NT // 2)]
        y_mm, y_taken = sc.sem("y_mm"), sc.sem("y_taken")
        with sc.block() as block:

            @block.tensor
            def _(pe):
                for t in range(NT):
                    nc.tensor.matmul(y_ps[t // 2][:, t % 2, :], srcT[:, t * P:(t + 1) * P], weights, start=True, stop=True).then_inc(y_mm, 1)

            @block.scalar
            def _(act):
                for i in range(NT // 2):
                    act.wait_ge(y_mm, ONE + 2 * i + 2)
                    src = y_ps[i][:, :, :]
                    if len(out.shape) == 4:
                        src = src.rearrange("p t (h d) -> p t h d", h=out.shape[2])
                    nc.scalar.activation(out[:, 2 * i:2 * i + 2], src, func).then_inc(y_taken, 1)


G4 = 4


def rotate_stage(nc, stage, Q, Q_swap, K, KR, KR_swap, cos, sin):
    def over_positions(table):
        return table[:, :].unsqueeze(1).to_broadcast([P, B, T])

    def batches(ap):
        return ap.rearrange("p (b t) -> p b t", b=B)

    with Scope(nc, stage) as sc:
        dve_step, pool_step, kr_ready = sc.sem("dve_step"), sc.sem("pool_step"), sc.sem("kr_ready")
        with sc.block() as block:

            @block.vector
            def _(dve):
                step = Steps(dve, dve_step)
                step.link(nc.vector.tensor_tensor(batches(KR[:, :]), batches(KR[:, :]), over_positions(cos), ALU.mult))
                dve.wait_ge(pool_step, ONE + 1)
                step.link(nc.vector.tensor_tensor(KR[:, :], KR[:, :], KR_swap[:, :], ALU.add))
                for g in range(G4):
                    nc.vector.tensor_tensor(K[:, g, :], K[:, g, :], KR[:, :], ALU.add).then_inc(kr_ready, 1)
                    step.link(nc.vector.tensor_tensor(batches(Q[:, g, :]), batches(Q[:, g, :]), over_positions(cos), ALU.mult))
                    dve.wait_ge(pool_step, ONE + g + 2)
                    step.link(nc.vector.tensor_tensor(Q[:, g, :], Q[:, g, :], Q_swap[:, g, :], ALU.add))

            @block.gpsimd
            def _(pool):
                nc.gpsimd.tensor_tensor(batches(KR_swap[:, :]), batches(KR_swap[:, :]), over_positions(sin), ALU.mult).then_inc(pool_step, 1)
                for g in range(G4):
                    nc.gpsimd.tensor_tensor(batches(Q_swap[:, g, :]), batches(Q_swap[:, g, :]), over_positions(sin), ALU.mult).then_inc(pool_step, 1)


NA = 8
R = 64
N2 = NA // 2


def losses_stage(nc, stage, xnT, encT, w_dec, b_dec, loss):
    N = 512
    work = [(n, m, c) for n2 in range(N2) for m in range(KD) for c in range(TOK // N) for n in (2 * n2, 2 * n2 + 1)]
    RING = 4
    with Scope(nc, stage) as sc:
        diff = [sc.sb(f"diff{i}", [P, N]) for i in range(RING)]
        square = [sc.sb(f"square{i}", [P, N]) for i in range(RING)]
        r_ps = [sc.ps(f"r_ps{i}", [P, N]) for i in range(RING)]
        r_mm, diff_ready, square_ready, sum_ready = (sc.sem(n) for n in ("r_mm", "diff_ready", "square_ready", "sum_ready"))
        with sc.block() as block:

            @block.tensor
            def _(pe):
                for i, (n, m, c) in enumerate(work):
                    if i >= RING:
                        pe.wait_ge(diff_ready, ONE + i - RING + 1)
                    rows = slice(n % 2 * R, (n % 2 + 1) * R)
                    nc.tensor.matmul(r_ps[i % RING][:, :], w_dec[rows, n // 2, m * P:(m + 1) * P], encT[rows, n // 2, c * N:(c + 1) * N], start=True, stop=True).then_inc(r_mm, 1)

            @block.vector
            def _(dve):
                def total(i):
                    n, m, c = work[i]
                    dve.wait_ge(square_ready, ONE + i + 1)
                    bs = slice(c * (N // T), (c + 1) * (N // T))
                    nc.vector.tensor_reduce(loss[:, n, m, bs], square[i % RING][:, :].rearrange("p (b t) -> p b t", t=T), AX.X, ALU.add).then_inc(sum_ready, 1)

                for i, (n, m, c) in enumerate(work):
                    dve.wait_ge(r_mm, ONE + i + 1)
                    if i >= RING:
                        dve.wait_ge(square_ready, ONE + i - RING + 1)
                    nc.vector.scalar_tensor_tensor(diff[i % RING][:, :], r_ps[i % RING][:, :], b_dec[:, m, n:n + 1], xnT[:, m, c * N:(c + 1) * N], ALU.add, ALU.subtract).then_inc(diff_ready, 1)
                    if i >= 2:
                        total(i - 2)
                total(len(work) - 2)
                total(len(work) - 1)

            @block.scalar
            def _(act):
                for i in range(len(work)):
                    act.wait_ge(diff_ready, ONE + i + 1)
                    if i >= RING:
                        act.wait_ge(sum_ready, ONE + i - RING + 1)
                    nc.scalar.activation(square[i % RING][:, :], diff[i % RING][:, :], ACT.Square).then_inc(square_ready, 1)


def choose_stage(nc, stage, loss, ones, adapter_ids, connected, b_up, b_base, pick, pick_rows, bias):
    with Scope(nc, stage) as sc:
        total = sc.sb("total", [P, NA, B])
        least = sc.sb("least", [P, B])
        chosen = sc.sb("chosen", [P, B])
        connected_f = sc.sb("connected_f", [P, NA])
        work = sc.sb("work", [P, KD, B, NA])
        l_ps = sc.ps("l_ps", [P, NA, KD, B])
        l_mm, dve_step = sc.sem("l_mm"), sc.sem("dve_step")

        def by_adapter(row):
            return row[:, :].unsqueeze(2).to_broadcast([P, NA, B])

        def by_batch(row):
            return row[:, :].unsqueeze(1).to_broadcast([P, NA, B])

        with sc.block() as block:

            @block.tensor
            def _(pe):
                nc.tensor.matmul(l_ps[:, :, :, :], ones[:, :], loss[:, :, :, :], start=True, stop=True).then_inc(l_mm, 1)

            @block.vector
            def _(dve):
                step = Steps(dve, dve_step)
                dve.wait_ge(l_mm, ONE + 1)
                step.link(nc.vector.tensor_copy(total[:, :, :], l_ps[:, :, 0, :]))
                step.link(nc.vector.tensor_tensor(total[:, :, :], total[:, :, :], l_ps[:, :, 1, :], ALU.add))
                step.link(nc.vector.tensor_reduce(least[:, :], total[:, :, :].rearrange("p n b -> p b n"), AX.X, ALU.min))
                step.link(nc.vector.tensor_tensor(total[:, :, :], total[:, :, :], by_batch(least), ALU.is_gt))
                step.link(nc.vector.tensor_scalar(total[:, :, :], total[:, :, :], float(NA), None, ALU.mult))
                step.link(nc.vector.tensor_tensor(total[:, :, :], total[:, :, :], by_adapter(adapter_ids), ALU.add))
                step.link(nc.vector.tensor_reduce(chosen[:, :], total[:, :, :].rearrange("p n b -> p b n"), AX.X, ALU.min))
                step.link(nc.vector.tensor_copy(connected_f[:, :], connected[:, :]))
                step.link(nc.vector.tensor_scalar(least[:, 0:NA], connected_f[:, :], 0.0, float(NA), ALU.is_lt, ALU.mult))
                step.link(nc.vector.tensor_tensor(connected_f[:, :], connected_f[:, :], least[:, 0:NA], ALU.add))
                step.link(nc.vector.tensor_scalar(connected_f[:, :], connected_f[:, :], 0.0, NA - 1.0, ALU.max, ALU.min))
                step.link(nc.vector.tensor_tensor(pick[:, :, :], by_adapter(adapter_ids), by_batch(chosen), ALU.is_equal))
                step.link(nc.vector.tensor_tensor(pick[:, :, :], pick[:, :, :], by_adapter(connected_f), ALU.mult))
                step.link(nc.vector.tensor_reduce(chosen[:, :], pick[:, :, :].rearrange("p n b -> p b n"), AX.X, ALU.add))
                step.link(nc.vector.tensor_tensor(pick[:, :, :], by_adapter(adapter_ids), by_batch(chosen), ALU.is_equal))
                for i in range(2):
                    rows = slice(i * R, (i + 1) * R)
                    step.link(nc.vector.tensor_copy(pick_rows[rows, :, :], pick[rows, i::2, :]))
                for m in range(KD):
                    step.link(nc.vector.tensor_tensor(work[:, m, :, :], pick[:, :, :].rearrange("p n b -> p b n"), b_up[:, m, :].unsqueeze(1).to_broadcast([P, B, NA]), ALU.mult))
                step.link(nc.vector.tensor_reduce(bias[:, :, :], work[:, :, :, :], AX.X, ALU.add))
                step.link(nc.vector.tensor_tensor(bias[:, :, :], bias[:, :, :], b_base[:, :].unsqueeze(2).to_broadcast([P, KD, B]), ALU.add))


def adapted_stage(nc, stage, X, xnT, midT, pick_rows, bias, w_base, w_up, ident, outT, out_d):
    N = 512
    work = [(m, c) for c in range(TOK // N) for m in range(KD)]
    with Scope(nc, stage) as sc:
        o_ps = [sc.ps(f"o_ps{i}", [P, N]) for i in range(len(work))]
        picked, o_mm, o_ready, stored = (sc.sem(n) for n in ("picked", "o_mm", "o_ready", "stored"))
        with sc.block() as block:

            @block.gpsimd
            def _(pool):
                for j in range(N2):
                    mid = midT[:, j, :].rearrange("p (b t) -> p b t", b=B)
                    nc.gpsimd.tensor_tensor(mid, mid, pick_rows[:, j, :].unsqueeze(2).to_broadcast([P, B, T]), ALU.mult).then_inc(picked, 1)

            @block.tensor
            def _(pe):
                def first(i, m, c):
                    for k in range(KD):
                        nc.tensor.matmul(o_ps[i][:, :], w_base[:, k, m * P:(m + 1) * P], xnT[:, k, c * N:(c + 1) * N], start=(k == 0), stop=False)
                    for t in range(N // P):
                        nc.tensor.matmul(o_ps[i][:, t * P:(t + 1) * P], X[:, c * (N // P) + t, m * P:(m + 1) * P], ident[:, :], start=False, stop=False)

                def second(i, m, c):
                    for j in range(N2):
                        pe.wait_ge(picked, ONE + j + 1)
                        mm = nc.tensor.matmul(o_ps[i][:, :], w_up[:, j, m * P:(m + 1) * P], midT[:, j, c * N:(c + 1) * N], start=False, stop=(j == N2 - 1))
                    mm.then_inc(o_mm, 1)

                for i, (m, c) in enumerate(work):
                    first(i, m, c)
                for i, (m, c) in enumerate(work):
                    second(i, m, c)

            @block.vector
            def _(dve):
                for i, (m, c) in enumerate(work):
                    dve.wait_ge(o_mm, ONE + i + 1)
                    bs = slice(c * (N // T), (c + 1) * (N // T))
                    nc.vector.tensor_tensor(outT[:, m, c * N:(c + 1) * N].rearrange("p (b t) -> p b t", t=T), o_ps[i][:, :].rearrange("p (b t) -> p b t", t=T),
                                            bias[:, m, bs].unsqueeze(2).to_broadcast([P, N // T, T]), ALU.add).then_inc(o_ready, 1)

            @block.sync
            def _(sp):
                for i, (m, c) in enumerate(work):
                    sp.wait_ge(o_ready, ONE + i + 1)
                    sp.dma_start(out_d[m * P:(m + 1) * P, c * N:(c + 1) * N], outT[:, m, c * N:(c + 1) * N]).then_inc(stored, 16)
                sp.wait_ge(stored, ONE + 16 * len(work))


def model(nc, d, out):
    with Scope(nc, "all") as sc:
        X = sc.sb("X", [P, NT, D])
        ident = sc.sb("ident", [P, P])
        mask16 = sc.sb("mask16", [P, HH])
        mask4 = sc.sb("mask4", [P, HH])
        eps = sc.sb("eps", [P, 1])
        ones = sc.sb("ones", [P, P])
        xnT = sc.sb("xnT", [P, KD, TOK])
        QT = sc.sb("QT", [P, KD, TOK])
        C_WoT = sc.sb("C_WoT", [P, KD, D])
        C_bo = sc.sb("C_bo", [1, D])
        expert_ids = sc.sb("expert_ids", [P, E])
        l0 = sc.stack.enter_context(Scope(nc, "l0"))
        names = ["A_WkT", "A_WvT", "A_WqT", "A_WoT", "R_Wq", "R_Wk", "R_Wv", "R_Wg", "R_Wo", "R_Wf1", "R_Wog1", "B_Wq", "B_Wk", "B_Wv", "B_Wo", "B_wr"]
        W = {n: l0.sb(n, [P, KD, d[n].shape[1]]) for n in names}
        rows = {n: l0.sb(n, list(d[n].shape)) for n in ["A_bo", "R_Wf2", "R_Wog2", "R_gain", "same_head", "head_of", "diag", "B_g1", "B_s1", "B_g2", "B_s2", "B_bq", "B_bk", "B_bv", "B_bo", "B_b2"]}
        upto = l0.sb("upto", [P, P], BF16)
        all_ones = l0.sb("all_ones", [P, P], BF16)
        b1 = l0.sb("b1", [P, E, KF])
        w1 = [l0.sb(f"w1_{j}", [P, KD, FF]) for j in range(2)]
        w2 = [l0.sb(f"w2_{j}", [P, KF, D]) for j in range(2)]
        w_in = [sc.stack.enter_context(nc.semaphore(f"w_in{j}")) for j in range(2)]
        loaded, cst = (sc.stack.enter_context(nc.semaphore(n)) for n in ("loaded", "cst"))
        start_semaphores(nc, sc.stack)
        with sc.block() as block:

            @block.sync
            def _(sp):
                n = 0
                for dst, src in [(X[:, :, :], d["x"].rearrange("(t p) d -> p t d", p=P)), (ident[:, :], d["ident"]), (mask16[:, :], d["mask16"]), (mask4[:, :], d["mask4"]), (C_bo[:, :], d["C_bo"]), (C_WoT[:, :, :], d["C_WoT"].rearrange("(k p) n -> p k n", p=P)), (upto[:, :], d["upto"]), (expert_ids[:, :], d["expert_ids"]),
                                 (b1[:, :, :], d["B_b1"].rearrange("p (e f) -> p e f", e=E))] \
                        + [(W[k][:, :, :], d[k].rearrange("(k p) n -> p k n", p=P)) for k in names] + [(rows[k][:, :], d[k]) for k in rows]:
                    sp.dma_start(dst, src).then_inc(loaded, 16)
                    n += 16
                for j in range(2):
                    sp.dma_start(w1[j][:, :, :], d["B_w1"][j].rearrange("(k p) f -> p k f", p=P)).then_inc(w_in[j], 16)
                    sp.dma_start(w2[j][:, :, :], d["B_w2"][j].rearrange("(k p) f -> p k f", p=P)).then_inc(w_in[j], 16)
                sp.wait_ge(loaded, n)

            @block.vector
            def _(dve):
                nc.vector.memset(eps[:, :], EPS).then_inc(cst, 1)
                nc.vector.memset(ones[:, :], 1.0).then_inc(cst, 1)
                nc.vector.memset(all_ones[:, :], 1.0).then_inc(cst, 1)

        def dump(X=X):
            stored = sc.sem("stored")
            with sc.block() as block:
                @block.sync
                def _(sp):
                    sp.dma_start(out.rearrange("(t p) d -> p t d", p=P), X[:, :, :]).then_inc(stored, 16)
                    sp.wait_ge(stored, ONE + 16)

        norm_stage(nc, "n0", X, ident, eps, xnT)
        project_stage(nc, "q0", half_jobs(W["A_WqT"], xnT, lambda m: [(QT[:, m, :], ACT.Copy, None)]))
        context_attention_stage(nc, "a0", X, QT, mask16, ident, d["ctxT"], None, W["A_WkT"], W["A_WvT"], W["A_WoT"], rows["A_bo"], ones)
        if STOP == 1:
            return dump()

        with Scope(nc, "rec") as rs:
            r = {n: rs.sb(n, [P, KD, TOK]) for n in ("q", "q_sig", "k", "k_sig", "v", "f", "gamma", "a")}
            low_f = rs.sb("low_f", [HD, TOK])
            low_g = rs.sb("low_g", [HD, TOK])
            gate = rs.sb("gate", [P, NT, D])
            history = r["q_sig"].rearrange("p m (a t) -> p (m a) t", t=T).rearrange("p (c h) t -> p c h t", c=4)
            gated = r["k_sig"].rearrange("p m (t d) -> p (m t) d", d=D)
            norm_stage(nc, "n1", X, ident, eps, xnT)
            project_stage(nc, "p1", [([(W[w][:, k, :], xnT[:, k, :]) for k in range(KD)], [(low[:, :], ACT.Copy, None)]) for w, low in (("R_Wf1", low_f), ("R_Wog1", low_g))])
            project_stage(nc, "p2",
                          half_jobs(W["R_Wq"], xnT, lambda m: [(r["q"][:, m, :], ACT.Copy, None), (r["q_sig"][:, m, :], ACT.Sigmoid, None)])
                          + half_jobs(W["R_Wk"], xnT, lambda m: [(r["k"][:, m, :], ACT.Copy, None), (r["k_sig"][:, m, :], ACT.Sigmoid, None)])
                          + half_jobs(W["R_Wv"], xnT, lambda m: [(r["v"][:, m, :], ACT.Copy, None)])
                          + half_jobs(W["R_Wg"], xnT, lambda m: [(r["gamma"][:, m, :], ACT.Sigmoid, None)])
                          + [([(rows["R_Wf2"][:, m * P:(m + 1) * P], low_f)], [(r["f"][:, m, :], ACT.Sigmoid, None)]) for m in range(KD)])
            token_product_stage(nc, "p3", low_g, rows["R_Wog2"][:, :], gate, ACT.Sigmoid)
            recurrence_inputs_stage(nc, "p4", r, rows["same_head"], gate)
            recurrence_stage(nc, "r1", r, rows["same_head"], rows["head_of"], rows["diag"], history)
            regroup_stage(nc, "r2", history, ident, gate, gated)
            norm_stage(nc, "n2", gated, ident, eps, gain=rows["R_gain"], product=(W["R_Wo"], None, None), add_to=X)
        if STOP == 2:
            return dump()


        with Scope(nc, "ffn") as fs:
            Y = fs.sb("Y", [P, NT, D])
            KT = fs.sb("KT", [P, KD, TOK])
            vals = fs.sb("vals", [P, NT, H, VA])
            norm_stage(nc, "n3", X, ident, eps, keep=Y)
            fill_stage(nc, "f3", vals[:, :, :, :], 1.0)
            norm_stage(nc, "n4", Y, ident, eps, xnT=xnT, gain=rows["B_g1"], shift=rows["B_s1"], product=(W["B_Wv"], rows["B_bv"], ones), heads_out=vals)
            project_stage(nc, "p5", half_jobs(W["B_Wq"], xnT, lambda m: [(QT[:, m, :], ACT.Identity, rows["B_bq"][:, m:m + 1])])
                          + half_jobs(W["B_Wk"], xnT, lambda m: [(KT[:, m, :], ACT.Identity, rows["B_bk"][:, m:m + 1])]))
            batch_attention_stage(nc, "a1", Y, QT, KT, vals, mask4, ident, W["B_Wo"], rows["B_bo"], ones)
            if STOP == 2.5:
                return dump(Y)
            xn = fs.sb("xn", [P, NT, D])
            slot, slot_kept = (fs.sb(n, [P, NT, 2], U32) for n in ("slot", "slot_kept"))
            weight = fs.sb("weight", [P, NT, 2])
            buf_d = nc.dram_tensor("expert_rows", (ROWS, D), F32, kind="Internal").ap()
            y_d = nc.dram_tensor("expert_out", (ROWS, D), F32, kind="Internal").ap()
            zeros = fs.sb("zeros", [P, 2 * D])
            fill_stage(nc, "f6", zeros[:, :], 0.0)
            norm_stage(nc, "n6", Y, ident, eps, xnT=xnT, gain=rows["B_g2"], shift=rows["B_s2"], keep=xn)
            routing_stage(nc, "m1", xnT, W["B_wr"], upto, all_ones, expert_ids, slot, slot_kept, weight)
            scatter_stage(nc, "m2", xn, slot_kept, zeros, buf_d)
            experts_stage(nc, "m3", d["B_w1"], d["B_w2"], buf_d, y_d, w1, w2, w_in, b1, rows["B_b2"], ones, rows["B_g2"], rows["B_s2"], ident)
            combine_stage(nc, "m4", X, Y, y_d, slot, weight)
        if STOP == 3:
            return dump()



        l0.stack.close()
        norm_stage(nc, "n7", X, ident, eps, xnT=xnT)
        context_attention_stage(nc, "a2", X, xnT, mask4, ident, d["ctxT"], d["ctx"], None, None, C_WoT, C_bo, ones)
        if STOP == 4:
            return dump()

        with Scope(nc, "mla") as ms:
            def weight(name, shape):
                return ms.sb(name, shape)
            small = {n: ms.sb(n, shape) for n, shape in dict(D_low=[P, KD, P], D_KR=[P, KD, 2 * P], D_UQ=[P, 2 * G4 * P], D_UK=[P, G4 * P], D_UV=[P, D], D_WO=[P, KD, D],
                                                              D_cos=[P, T], D_sin=[P, T], D_causal=[P, T], D_mask=[P, G4]).items()}
            w_loaded = ms.sem("loaded")
            lowT = ms.sb("lowT", [P, TOK])
            Q, Q_swap, K = (ms.sb(n, [P, G4, TOK]) for n in ("Q", "Q_swap", "K"))
            KR, KR_swap = (ms.sb(n, [P, TOK]) for n in ("KR", "KR_swap"))
            vals = ms.sb("vals", [P, NT, H, VA])
            load_stage(nc, "l8", small, d, w_loaded)
            fill_stage(nc, "f8", vals[:, :, :, :], 1.0)
            norm_stage(nc, "n8", X, ident, eps, xnT=xnT)
            project_stage(nc, "p8", half_jobs(small["D_low"], xnT, lambda m: [(lowT[:, :], ACT.Copy, None)])
                          + half_jobs(small["D_KR"], xnT, lambda m: [((KR, KR_swap)[m][:, :], ACT.Copy, None)]))
            project_stage(nc, "p9", [([(small["D_UQ"][:, i * P:(i + 1) * P], lowT)], [((Q, Q_swap)[i // G4][:, i % G4, :], ACT.Copy, None)]) for i in range(2 * G4)]
                          + [([(small["D_UK"][:, i * P:(i + 1) * P], lowT)], [(K[:, i, :], ACT.Copy, None)]) for i in range(G4)])
            token_product_stage(nc, "p10", lowT, small["D_UV"][:, :], vals[:, :, :, 0:HD], ACT.Copy)
            rotate_stage(nc, "p11", Q, Q_swap, K, KR, KR_swap, small["D_cos"], small["D_sin"])
            batch_attention_stage(nc, "a3", X, Q, K, vals, small["D_mask"], ident, small["D_WO"], None, ones, clip=80.0, scale=float(1 / (HD + HD // 2) ** 0.5), causal=small["D_causal"])
        if STOP == 5:
            return dump()

        with Scope(nc, "ada") as fs:
            small = {n: fs.sb(n, shape) for n, shape in dict(F_enc=[P, KD, NA * R], F_down=[P, KD, NA * R], F_dec=[P, N2, D], F_up=[P, N2, D], F_base=[P, KD, D], F_benc=[P, N2], F_bdown=[P, N2],
                                                              F_bdec=[P, KD, NA], F_bup=[P, KD, NA], F_bbase=[P, KD]).items()}
            connected = fs.sb("connected", [P, NA], I32)
            small["F_connected"] = connected
            w_loaded = fs.sem("loaded")
            encT, midT = (fs.sb(n, [P, N2, TOK]) for n in ("encT", "midT"))
            loss = fs.sb("loss", [P, NA, KD, B])
            pick = fs.sb("pick", [P, NA, B])
            pick_rows = fs.sb("pick_rows", [P, N2, B])
            bias = fs.sb("bias", [P, KD, B])
            outT = fs.sb("outT", [P, KD, TOK])
            load_stage(nc, "l12", small, d, w_loaded)
            norm_stage(nc, "n12", X, ident, eps, xnT=xnT)
            project_stage(nc, "p12", half_jobs(small["F_enc"], xnT, lambda j: [(encT[:, j, :], ACT.Relu, small["F_benc"][:, j:j + 1])])
                          + half_jobs(small["F_down"], xnT, lambda j: [(midT[:, j, :], ACT.Relu, small["F_bdown"][:, j:j + 1])]))
            losses_stage(nc, "p13", xnT, encT, small["F_dec"], small["F_bdec"], loss)
            choose_stage(nc, "p14", loss, ones, expert_ids, connected, small["F_bup"], small["F_bbase"], pick, pick_rows, bias)
            adapted_stage(nc, "p15", X, xnT, midT, pick_rows, bias, small["F_base"], small["F_up"], ident, outT, out)


STOP = 6


def kernel(**inputs):
    import numpy as np
    import concourse.bacc as bacc
    from concourse.bass_utils import run_bass_kernel_spmd

    f = {k: np.asarray(v) for k, v in inputs.items()}
    p = np.arange(P)
    a = {
        "x": f["x"].reshape(TOK, D),
        "ctxT": f["ctx_1024"].transpose(0, 2, 1),
        "ident": np.eye(P, dtype=np.float32),
        "mask16": (p[:, None] // HD == np.arange(HH)).astype(np.float32) / 16,
        "mask4": (p[:, None] // HD == np.arange(HH)).astype(np.float32) / 4,
        "A_WqT": f["L0_xattn_Wq"].T, "A_WkT": f["L0_xattn_Wk"].T, "A_WvT": f["L0_xattn_Wv"].T, "A_WoT": f["L0_xattn_Wo"].T,
        "A_bo": f["L0_xattn_bo"].reshape(1, D),
        "same_head": (p[:, None] // HD == p // HD).astype(np.float32), "head_of": (p[:, None] // HD == np.arange(HH)).astype(np.float32),
        "diag": (p[:, None] % HD == np.arange(HD)).astype(np.float32),
        "R_Wq": f["L0_attn_Wq"], "R_Wk": f["L0_attn_Wk"], "R_Wv": f["L0_attn_Wv"], "R_Wg": np.repeat(f["L0_attn_Wgamma"], HD, axis=1), "R_Wo": f["L0_attn_Wo"],
        "R_Wf1": f["L0_attn_Wf1"], "R_Wog1": f["L0_attn_Wog1"], "R_Wf2": f["L0_attn_Wf2"], "R_Wog2": f["L0_attn_Wog2"],
        "upto": np.triu(np.ones((P, P))).astype("bfloat16"), "expert_ids": np.tile(np.arange(E, dtype=np.float32), (P, 1)),
        "B_wr": f["L0_ffn_wr"], "B_w1": f["L0_ffn_w1"], "B_w2": f["L0_ffn_w2"], "B_b2": f["L0_ffn_b2"].reshape(1, E, D),
        "B_b1": f["L0_ffn_b1"].reshape(E, KF, P).transpose(2, 0, 1).reshape(P, E * KF),
        "B_Wq": f["L0_ffn_wq"], "B_Wk": f["L0_ffn_wk"], "B_Wv": f["L0_ffn_wv"], "B_Wo": f["L0_ffn_wo"],
        **{"B_" + n: f["L0_ffn_" + o].reshape(KD, P).T for n, o in (("g1", "ln1_g"), ("s1", "ln1_b"), ("g2", "ln2_g"), ("s2", "ln2_b"), ("bq", "bq"), ("bk", "bk"))},
        "B_bv": f["L0_ffn_bv"].reshape(1, D), "B_bo": f["L0_ffn_bo"].reshape(1, D),
        "R_gain": f["L0_attn_norm_w"].reshape(KD, P).T,
        "C_WoT": f["L1_xattn_w_proj"].T, "C_bo": f["L1_xattn_b_proj"].reshape(1, D),
    }

    def slots(w, lo):
        out = np.zeros((w.shape[0], H, 32), np.float32)
        out[:, :, lo:lo + w.shape[1] // H] = w.reshape(w.shape[0], H, -1)
        return out.reshape(w.shape[0], H * 32)

    def swap(w):
        return w.reshape(w.shape[0], -1, 2)[:, :, ::-1].reshape(w.shape)

    HR = HD // 2
    upper, lower = (lambda w: np.concatenate([w, np.zeros_like(w)])), (lambda w: np.concatenate([np.zeros_like(w), w]))
    qr, kr = f["L1_attn_W_QR"], f["L1_attn_W_KR"]
    heads_kr = lambda w: slots(np.tile(w, (1, H)), HD)[:, 0:P]
    angle = (10000.0 ** (-np.arange(0, HR, 2, dtype=np.float32) / np.float32(HR))).astype(np.float32)[:, None] * np.arange(T, dtype=np.float32)
    cos, sin = np.zeros((32, T), np.float32), np.zeros((32, T), np.float32)
    cos[0:HD] = 1
    cos[HD:HD + HR] = np.repeat(np.cos(angle), 2, axis=0)
    sin[HD:HD + HR] = np.repeat(np.sin(angle), 2, axis=0) * np.tile([[-1.0], [1.0]], (HR // 2, 1))
    a |= {
        "ctx": f["ctx_1024"],
        "D_low": np.concatenate([f["L1_attn_W_DQ"], f["L1_attn_W_DKV"]], axis=1),
        "D_UQ": upper(np.concatenate([slots(f["L1_attn_W_UQ"], 0) + slots(qr, HD), slots(swap(qr), HD)], axis=1)),
        "D_UK": lower(slots(f["L1_attn_W_UK"], 0)), "D_UV": lower(f["L1_attn_W_UV"]),
        "D_KR": np.concatenate([heads_kr(kr), heads_kr(swap(kr))], axis=1), "D_WO": f["L1_attn_W_O"],
        "D_cos": np.tile(cos, (4, 1)), "D_sin": np.tile(sin, (4, 1)),
        "D_causal": np.tile(np.tri(T, dtype=np.float32), (2, 1)), "D_mask": (p[:, None] // 32 == np.arange(4)).astype(np.float32),
        "F_enc": f["L1_ffn_W_enc"].transpose(1, 0, 2).reshape(D, NA * R), "F_down": f["L1_ffn_W_down"].transpose(1, 0, 2).reshape(D, NA * R),
        "F_dec": f["L1_ffn_W_dec"].reshape(NA * R, D), "F_up": f["L1_ffn_W_up"].reshape(NA * R, D), "F_base": f["L1_ffn_W_base"],
        "F_benc": f["L1_ffn_b_enc"].reshape(N2, P).T, "F_bdown": f["L1_ffn_b_down"].reshape(N2, P).T,
        "F_bdec": f["L1_ffn_b_dec"].T, "F_bup": f["L1_ffn_b_up"].T,
        "F_bbase": f["L1_ffn_b_base"].reshape(KD, P).T, "F_connected": np.tile(f["L1_ffn_connected_idx"], (P, 1)),
    }
    nc = bacc.Bacc("TRN2", target_bir_lowering=False, num_devices=1)
    arrays, d = {}, {}
    for name, v in a.items():
        v = np.ascontiguousarray(v)
        arrays["in_" + name] = v
        d[name] = nc.dram_tensor("in_" + name, v.shape, mybir.dt.from_np(v.dtype), kind="ExternalInput").ap()
    out = nc.dram_tensor("out", (TOK, D) if STOP < 6 else (D, TOK), F32, kind="ExternalOutput").ap()
    model(nc, d, out)
    r = run_bass_kernel_spmd(nc, [arrays], core_ids=[0])
    return np.ascontiguousarray(r.results[0]["out"].T).reshape(B, T, D)
```
